# Optimizing a Trainium2 kernel written in Bass

```python
import numpy as np
import jax
import jax.numpy as jnp

def _softmax(x, axis=-1):
    return jax.nn.softmax(x, axis=axis)

def _gelu(x):
    return jax.nn.gelu(x, approximate=True)

def _silu(x):
    return jax.nn.silu(x)

def _sigmoid(x):
    return jax.nn.sigmoid(x)

def _layernorm(x, axis=-1, eps=1e-05):
    m = jnp.mean(x, axis=axis, keepdims=True)
    v = jnp.var(x, axis=axis, keepdims=True)
    return (x - m) / jnp.sqrt(v + eps)

def _scatter_add(tgt, idx, src, axis=0):
    return tgt.at[idx].add(src)

def _segment_sum(src, seg, n):
    return jax.ops.segment_sum(src, seg, n)
kernel_name = 'mk_gnn_preln_d2_gnn_r8_e0a30c'

def setup_inputs(seed: int=0):
    np.random.seed(seed)
    _w = jnp.asarray

    def _rec_inputs():
        import jax
        import jax.numpy as jnp
        _gk = jax.random.key(seed)
        x = -0.0005121 + 1.001 * jax.random.normal(jax.random.fold_in(_gk, 1), (6250, 64), jnp.float32)
        _s = jax.random.randint(jax.random.fold_in(_gk, 2), (100000,), 0, 6250, jnp.int32)
        _d = jax.random.randint(jax.random.fold_in(_gk, 3), (100000,), 0, 6250, jnp.int32)
        _loop = jnp.arange(6250, dtype=jnp.int32)
        src = jnp.concatenate([_s, _d, _loop])
        dst = jnp.concatenate([_d, _s, _loop])
        _o = jnp.argsort(dst, stable=True)
        src = src[_o]
        dst = dst[_o]
        edge_attr3_2x64 = jax.random.uniform(jax.random.fold_in(_gk, 12), (206250, 2, 64), jnp.float32, 0.0, 1)
        return (x, src, dst, edge_attr3_2x64)
    x, src, dst, edge_attr3_2x64 = _rec_inputs()

    def _L0_gnn_setup():
        import jax, jax.numpy as jnp
        import numpy as np
        N_NODES = 6250
        N_EDGES = 100000
        IN_FEAT = 64
        OUT_FEAT = 64
        key = jax.random.key(seed)
        k_h, k_src, k_dst, k_w = jax.random.split(key, 4)
        h = jax.random.normal(k_h, (N_NODES, IN_FEAT), dtype=jnp.float32)
        src = jax.random.randint(k_src, (N_EDGES,), 0, N_NODES, dtype=jnp.int64)
        dst = jax.random.randint(k_dst, (N_EDGES,), 0, N_NODES, dtype=jnp.int64)
        W = jax.random.normal(k_w, (2 * IN_FEAT, OUT_FEAT), dtype=jnp.float32) * (1.0 / np.sqrt(2 * IN_FEAT))
        b = jnp.zeros((OUT_FEAT,), dtype=jnp.float32)
        return {'h': h, 'src': src, 'dst': dst, 'W': W, 'b': b}
    _L0_gnn_all = _L0_gnn_setup()
    _L0_gnn_in = {k: v for k, v in _L0_gnn_all.items() if k in ('W', 'b')}
    del _L0_gnn_all

    def _L1_gnn_setup():
        import jax, jax.numpy as jnp
        import numpy as np
        BETA = 0.2
        GAMMA = 0.95
        N_NODES = 12500
        N_EDGES = 200000
        D = 64
        key = jax.random.key(seed)
        k1, k2, k3, k4 = jax.random.split(key, 4)
        z = jax.random.normal(k1, (N_NODES, D), dtype=jnp.float32)
        e = jax.random.uniform(k2, (N_EDGES, 2, D), dtype=jnp.float32)
        src = jax.random.randint(k3, (N_EDGES,), 0, N_NODES, dtype=jnp.int64)
        dst = jax.random.randint(k4, (N_EDGES,), 0, N_NODES, dtype=jnp.int64)
        return {'z': z, 'e': e, 'src': src, 'dst': dst}
    _L1_gnn_all = _L1_gnn_setup()
    _L1_gnn_in = {k: v for k, v in _L1_gnn_all.items() if k in ()}
    del _L1_gnn_all
    return {'x': x, 'src': src, 'dst': dst, 'edge_attr3_2x64': edge_attr3_2x64, 'L0_gnn_W': _L0_gnn_in['W'], 'L0_gnn_b': _L0_gnn_in['b']}

def reference(x, src, dst, edge_attr3_2x64, L0_gnn_W, L0_gnn_b):
    import jax
    import jax.numpy as jnp

    def _L0_gnn_ref(h, src, dst, W, b):
        import jax, jax.numpy as jnp
        import numpy as np
        N_NODES = 6250
        N_EDGES = 100000
        IN_FEAT = 64
        OUT_FEAT = 64
        msgs = h[src]
        summed = jax.ops.segment_sum(msgs, dst, num_segments=N_NODES)
        deg = jax.ops.segment_sum(jnp.ones((src.shape[0],), h.dtype), dst, num_segments=N_NODES)
        h_N = summed / jnp.maximum(deg, 1.0)[:, None]
        h_total = jnp.concatenate([h, h_N], axis=1)
        return h_total @ W + b

    def _L1_gnn_ref(z, e, src, dst):
        import jax, jax.numpy as jnp
        import numpy as np
        BETA = 0.2
        GAMMA = 0.95
        N_NODES = 12500
        N_EDGES = 200000
        D = 64
        n = z.shape[0]
        zmax = jnp.max(z, axis=-1, keepdims=True)
        e0 = e[:, 0, :]
        e1 = e[:, 1, :]
        q = GAMMA * zmax[src] * e1 + e0
        sum_q = jax.ops.segment_sum(q, dst, num_segments=n)
        sum_ac = jax.ops.segment_sum(e1, dst, num_segments=n)
        z_new = BETA * z + (1.0 - BETA) * sum_q / (sum_ac + 1e-06)
        deg = jax.ops.segment_sum(jnp.ones(dst.shape, dtype=z.dtype), dst, num_segments=n)
        return jnp.where(deg[:, None] > 0, z_new, z)
    h = jnp.maximum(_layernorm(x, axis=-1), 0.0)
    x = x + _L0_gnn_ref(h, src, dst, L0_gnn_W, L0_gnn_b)
    h = jnp.maximum(_layernorm(x, axis=-1), 0.0)
    x = x + _L1_gnn_ref(h, edge_attr3_2x64, src, dst)
    return x

_drawn_inputs = setup_inputs


def setup_inputs(seed=0):
    import zlib

    import numpy as np

    out = dict(_drawn_inputs(seed))
    spreads = {'L0_gnn_b': (0.0, 0.1)}
    factors = {}
    for name, (base, spread) in spreads.items():
        noise = np.random.default_rng([zlib.crc32(name.encode()), seed]).standard_normal(out[name].shape)
        drawn = base * np.exp(spread * noise) if base else spread * noise
        out[name] = jnp.asarray(drawn.astype(out[name].dtype))
    for name, factor in factors.items():
        out[name] = (out[name] * factor).astype(out[name].dtype)
    return out
```

```python
from contextlib import ExitStack

import concourse.bass as bass
from concourse import mybir
from concourse.alu_op_type import AluOpType as ALU

ACT = mybir.ActivationFunctionType
AX = mybir.AxisListType
F32 = mybir.dt.float32
BF16 = mybir.dt.bfloat16
I32 = mybir.dt.int32
U32 = mybir.dt.uint32

P = 128
N = 6250
E = 206250
D = 64
F2 = 2 * D
T = (N + P - 1) // P
NP = T * P
TAIL = N - (T - 1) * P
H1 = D + 1
EPS = 1e-5
BETA = 0.2
GAMMA = 0.95

GC = 125
GN = E // GC
TG = 7
assert GC * GN == E and T % TG == 0


def layernorm_relu(nc, dve, act_done, dve_done, xin, hout, tmp, stat, n):
    steps = [n]

    def step(ins):
        steps[0] += 1
        ins.then_inc(dve_done, 1)
        dve.wait_ge(dve_done, steps[0])

    mean, ssq, rstd = stat[:, 0, :], stat[:, 1, :], stat[:, 3, :]
    step(nc.vector.reduce_sum(mean, xin, AX.X))
    step(nc.vector.tensor_scalar(mean, mean, 1.0 / D, None, ALU.mult))
    step(nc.vector.tensor_tensor(hout, xin, mean.unsqueeze(2).to_broadcast([P, T, D]), ALU.subtract))
    return step, ssq, rstd


def build(nc, x, src, dst, edge, W, b, out):
    ctx = ExitStack()
    with ctx:
        def sb(name, shape, dt=F32):
            return ctx.enter_context(nc.sbuf_tensor(name, shape, dt))

        def sem(name):
            return ctx.enter_context(nc.semaphore(name))

        mem = dict(
            xs=sb("xs", [P, T, D]), h=sb("h", [P, T, H1]), tmp=sb("tmp", [P, T, D]), stat=sb("stat", [P, 4, T]),
            ident=sb("ident", [P, P]), W=sb("W_sb", [P, D]), bias=sb("bias", [P, D]),
            sums=sb("sums", [P, T, F2]), z=sb("z", [P, T]), deg=sb("deg", [P, T]), eps=sb("eps", [P, 1]))
        for name, shape in (("h_dram", [NP, H1]), ("acc1_dram", [NP, H1]), ("z_dram", [NP, 1]), ("acc2_dram", [NP, F2])):
            mem[name] = nc.dram_tensor(name, shape, F32).ap()
        prepare(nc, ctx, sem, mem, x, W, b)
        general_sums(nc, ctx, sem, sb, mem, src, dst, edge, 1)
        update_nodes(nc, ctx, sem, sb, mem)
        general_sums(nc, ctx, sem, sb, mem, src, dst, edge, 2)
        write_result(nc, ctx, sem, sb, mem, out)


def prepare(nc, ctx, sem, m, x, W, b):
    tail_zero, x_in, w_in = sem("tail_zero"), sem("x_in"), sem("w_in")
    id_zero, id_done = sem("id_zero"), sem("id_done")
    xv = x[0:(T - 1) * P, :].rearrange("(t p) f -> p t f", p=P)
    ln_dve, ln_act = sem("ln1_dve"), sem("ln1_act")
    eps_set, ones_set = sem("eps_set"), sem("ones_set")
    with nc.Block() as block:
        @block.sync
        def _(sp):
            sp.dma_start(m["xs"][:, 0:T - 1, :], xv).then_inc(x_in, 16)
            sp.wait_ge(tail_zero, 1)
            sp.dma_start(m["xs"][0:TAIL, T - 1, :], x[(T - 1) * P:N, :]).then_inc(x_in, 16)
            sp.dma_start(m["W"][:], W).then_inc(w_in, 16)
            sp.dma_start(m["bias"][:], b.rearrange("(o f) -> o f", o=1).to_broadcast([P, D])).then_inc(w_in, 16)
            sp.wait_ge(w_in, 32)

        @block.gpsimd
        def _(pool):
            nc.gpsimd.memset(m["xs"][:, T - 1, :], 0.0).then_inc(tail_zero, 1)
            nc.gpsimd.memset(m["eps"][:], EPS).then_inc(eps_set, 1)
            nc.gpsimd.memset(m["h"][:, :, D:H1], 1.0).then_inc(ones_set, 1)
            nc.gpsimd.memset(m["ident"][:], 0.0).then_inc(id_zero, 1)
            pool.wait_ge(id_zero, 1)
            nc.gpsimd.affine_select(out=m["ident"][:], in_=m["ident"][:], compare_op=ALU.not_equal, fill=1.0,
                                    base=0, pattern=[[-1, P]], channel_multiplier=1).then_inc(id_done, 1)

        @block.vector
        def _(dve):
            dve.wait_ge(x_in, 32)
            normalize_dve(nc, dve, ln_dve, ln_act, m["xs"][:], m["h"][:, :, 0:D], m)

        @block.scalar
        def _(act):
            act.wait_ge(eps_set, 1)
            normalize_act(nc, act, ln_dve, ln_act, m["h"][:, :, 0:D], m)


def normalize_dve(nc, dve, ln_dve, ln_act, xin, hout, m):
    mean, ssq, std, rstd = (m["stat"][:, i, :] for i in range(4))
    nc.vector.reduce_sum(ssq, xin, AX.X).then_inc(ln_dve, 1)
    dve.wait_ge(ln_dve, 1)
    nc.vector.tensor_scalar(mean, ssq, 1.0 / D, None, ALU.mult).then_inc(ln_dve, 1)
    dve.wait_ge(ln_dve, 2)
    nc.vector.tensor_tensor(hout, xin, mean.unsqueeze(2).to_broadcast([P, T, D]), ALU.subtract).then_inc(ln_dve, 1)
    dve.wait_ge(ln_act, 1)
    nc.vector.reduce_sum(ssq, m["tmp"][:], AX.X).then_inc(ln_dve, 1)
    dve.wait_ge(ln_act, 2)
    nc.vector.reciprocal(rstd, std).then_inc(ln_dve, 1)
    dve.wait_ge(ln_dve, 5)
    nc.vector.scalar_tensor_tensor(out=hout, in0=hout, scalar=0.0, in1=rstd.unsqueeze(2).to_broadcast([P, T, D]),
                                   op0=ALU.max, op1=ALU.mult).then_inc(ln_dve, 1)


def normalize_act(nc, act, ln_dve, ln_act, hout, m):
    act.wait_ge(ln_dve, 3)
    nc.scalar.activation(m["tmp"][:], hout, ACT.Square).then_inc(ln_act, 1)
    act.wait_ge(ln_dve, 4)
    nc.scalar.activation(m["stat"][:, 2, :], m["stat"][:, 1, :], ACT.Sqrt, bias=m["eps"][:], scale=1.0 / D).then_inc(ln_act, 1)


def general_sums(nc, ctx, sem, sb, m, src, dst, edge, layer):
    R = H1 if layer == 1 else F2
    n = f"g{layer}_"
    acc = m["acc1_dram"] if layer == 1 else m["acc2_dram"]
    idx = sb(n + "idx", [GC, 2], I32)
    dstf = sb(n + "dstf", [GC, 1])
    same = sb(n + "same", [GC, GC])
    vals = sb(n + "vals", [GC, R])
    old = sb(n + "old", [GC, R])
    new = sb(n + "new", [GC, R])
    zero = sb(n + "zero", [P, R])
    zsrc = sb(n + "zsrc", [GC, 1])
    dst_row = ctx.enter_context(nc.psum_tensor(n + "dst_row", [GC, GC], F32))
    total = ctx.enter_context(nc.psum_tensor(n + "total", [GC, R], F32))
    names = ["zeroed", "table_out", "acc_zeroed", "acc_written", "idx_in", "edge_in", "rows_in", "dst_cast", "row_ready",
             "same_ready", "vals_ready", "scaled", "sum_ready", "new_ready", "sums_in",
             "gather_begun", "scatter_begun"]
    s = {k: sem(n + k) for k in names}
    srcv = src.rearrange("(c o) -> c o", o=1)
    dstv = dst.rearrange("(c o) -> c o", o=1)
    edgev = edge.rearrange("e a f -> e (a f)")
    per_chunk_loads = 32
    rows_per_chunk = 32
    with nc.Block() as block:
        @block.sync
        def _(sp):
            if layer == 1:
                sp.dma_start(m["h_dram"].rearrange("(t p) f -> p t f", p=P), m["h"][:]).then_inc(s["table_out"], 16)
            else:
                sp.dma_start(m["z_dram"].rearrange("(t p) o -> p t o", p=P), m["z"][:].unsqueeze(2), allow_slow_non_contiguous=True).then_inc(s["table_out"], 16)
            sp.wait_ge(s["zeroed"], 1)
            sp.dma_start(acc.rearrange("(t p) f -> p t f", p=P), zero[:].unsqueeze(1).to_broadcast([P, T, R])).then_inc(s["acc_zeroed"], 16)
            sp.wait_ge(s["acc_zeroed"], 16)
            sp.wait_ge(s["table_out"], 16)

            def load(i):
                sp.dma_start(idx[:, 0:1], srcv[bass.ds(i * GC, GC), :]).then_inc(s["idx_in"], 16)
                sp.dma_start(idx[:, 1:2], dstv[bass.ds(i * GC, GC), :]).then_inc(s["idx_in"], 16)
                if layer == 2:
                    sp.dma_start(vals[:], edgev[bass.ds(i * GC, GC), :]).then_inc(s["edge_in"], 16)

            load(0)
            with sp.Fori(1, GN) as i:
                sp.wait_ge(s["acc_written"], 16 * i)
                load(i)
            sp.wait_ge(s["acc_written"], 16 * GN)
            out = m["sums"][:, :, 0:R]
            sp.dma_start(out, acc.rearrange("(t p) f -> p t f", p=P)).then_inc(s["sums_in"], 16)
            sp.wait_ge(s["sums_in"], 16)

        @block.gpsimd
        def _(pool):
            nc.gpsimd.memset(zero[:], 0.0).then_inc(s["zeroed"], 1)
            with pool.Fori(0, GN) as i:
                pool.wait_ge(s["idx_in"], 32 * i + 32)
                pool.sem_inc(s["gather_begun"], 1)
                if layer == 1:
                    pool.indirect_dma_start(vals[:], None, m["h_dram"], bass.IndirectOffsetOnAxis(idx[:, 0:1].bitcast(U32), 0)).then_inc(s["rows_in"], 16)
                else:
                    pool.indirect_dma_start(zsrc[:], None, m["z_dram"], bass.IndirectOffsetOnAxis(idx[:, 0:1].bitcast(U32), 0)).then_inc(s["rows_in"], 16)
                pool.indirect_dma_start(old[:], None, acc, bass.IndirectOffsetOnAxis(idx[:, 1:2].bitcast(U32), 0)).then_inc(s["rows_in"], 16)
                pool.wait_ge(s["new_ready"], i + 1)
                pool.sem_inc(s["scatter_begun"], 1)
                pool.indirect_dma_start(acc, bass.IndirectOffsetOnAxis(idx[:, 1:2].bitcast(U32), 0), new[:], None).then_inc(s["acc_written"], 16)

        @block.vector
        def _(dve):
            with dve.Fori(0, GN) as i:
                dve.wait_ge(s["idx_in"], 32 * i + 32)
                nc.vector.tensor_copy(dstf[:], idx[:, 1:2]).then_inc(s["dst_cast"], 1)
                dve.wait_ge(s["row_ready"], i + 1)
                nc.vector.tensor_scalar(same[:], dst_row[:], dstf[:], None, ALU.is_equal).then_inc(s["same_ready"], 1)
                dve.wait_ge(s["rows_in"], 32 * i + 32)
                if layer == 2:
                    dve.wait_ge(s["edge_in"], 16 * i + 16)
                    nc.vector.scalar_tensor_tensor(out=vals[:, 0:D], in0=vals[:, D:F2], scalar=zsrc[:], in1=vals[:, 0:D],
                                                   op0=ALU.mult, op1=ALU.add).then_inc(s["vals_ready"], 1)
                dve.wait_ge(s["sum_ready"], i + 1)
                nc.vector.tensor_tensor(new[:], total[:], old[:], ALU.add).then_inc(s["new_ready"], 1)

        @block.tensor
        def _(pe):
            with pe.Fori(0, GN) as i:
                pe.wait_ge(s["dst_cast"], i + 1)
                nc.tensor.matmul(dst_row[:], dstf[:].to_broadcast([GC, GC]), m["ident"][0:GC, 0:GC], start=True, stop=True).then_inc(s["row_ready"], 1)
                pe.wait_ge(s["same_ready"], i + 1)
                if layer == 1:
                    pe.wait_ge(s["rows_in"], 32 * i + 32)
                else:
                    pe.wait_ge(s["vals_ready"], i + 1)
                nc.tensor.matmul(total[:], same[:], vals[:], start=True, stop=True).then_inc(s["sum_ready"], 1)


def update_nodes(nc, ctx, sem, sb, m):
    cat = sb("cat", [P, TG, F2])
    catT = sb("catT", [P, TG, P])
    rdeg = sb("rdeg", [P, T])
    psT = ctx.enter_context(nc.psum_tensor("psT", [P, 8, P], F32))
    psY = ctx.enter_context(nc.psum_tensor("psY", [P, 8, D], F32))
    deg_done, rdeg_done, bias_added, h_copied, n_scaled = (sem(k) for k in ("deg_done", "rdeg_done", "bias_added", "h_copied", "n_scaled"))
    turned, turned_out, projected, x_updated = (sem(k) for k in ("turned", "turned_out", "projected", "x_updated"))
    ln_dve, ln_act, z_max = sem("ln2_dve"), sem("ln2_act"), sem("z_max")
    with nc.Block() as block:
        @block.vector
        def _(dve):
            nc.vector.tensor_copy(m["deg"][:].unsqueeze(2), m["sums"][:, :, D:H1]).then_inc(deg_done, 1)
            dve.wait_ge(deg_done, 1)
            nc.vector.tensor_scalar(rdeg[:], m["deg"][:], 1.0, None, ALU.max).then_inc(rdeg_done, 1)
            dve.wait_ge(rdeg_done, 1)
            nc.vector.reciprocal(rdeg[:], rdeg[:]).then_inc(rdeg_done, 1)
            nc.vector.tensor_tensor(m["xs"][:], m["xs"][:], m["bias"][:].unsqueeze(1).to_broadcast([P, T, D]), ALU.add).then_inc(bias_added, 1)
            dve.wait_ge(rdeg_done, 2)
            nc.vector.tensor_tensor(m["sums"][:, :, 0:D], m["sums"][:, :, 0:D], rdeg[:].unsqueeze(2).to_broadcast([P, T, D]), ALU.mult).then_inc(n_scaled, 1)
            dve.wait_ge(bias_added, 1)
            dve.wait_ge(n_scaled, 1)
            with dve.Fori(0, T // TG) as g:
                nc.vector.tensor_copy(cat[:, :, 0:D], m["h"][:, bass.ds(g * TG, TG), 0:D]).then_inc(h_copied, 1)
                nc.vector.tensor_copy(cat[:, :, D:F2], m["sums"][:, bass.ds(g * TG, TG), 0:D]).then_inc(h_copied, 1)
                dve.wait_ge(projected, g + 1)
                xg = m["xs"][:, bass.ds(g * TG, TG), :]
                nc.vector.tensor_tensor(xg, xg, psY[:, 0:TG, :], ALU.add).then_inc(x_updated, 1)
            dve.wait_ge(x_updated, T // TG)
            normalize_dve(nc, dve, ln_dve, ln_act, m["xs"][:], m["h"][:, :, 0:D], m)
            dve.wait_ge(ln_dve, 6)
            nc.vector.tensor_reduce(m["z"][:], m["h"][:, :, 0:D], AX.X, ALU.max).then_inc(z_max, 1)
            dve.wait_ge(z_max, 1)
            nc.vector.tensor_scalar(m["z"][:], m["z"][:], GAMMA, None, ALU.mult).then_inc(z_max, 1)

        @block.tensor
        def _(pe):
            with pe.Fori(0, T // TG) as g:
                pe.wait_ge(h_copied, 2 * g + 2)
                for k in range(TG):
                    last = nc.tensor.transpose(psT[:, k, :], cat[:, k, :], m["ident"][:])
                last.then_inc(turned, 1)
                pe.wait_ge(turned_out, g + 1)
                for k in range(TG):
                    last = nc.tensor.matmul(psY[:, k, :], catT[:, k, :], m["W"][:], start=True, stop=True)
                last.then_inc(projected, 1)

        @block.scalar
        def _(act):
            with act.Fori(0, T // TG) as g:
                act.wait_ge(turned, g + 1)
                nc.scalar.copy(catT[:], psT[:, 0:TG, :]).then_inc(turned_out, 1)
            normalize_act(nc, act, ln_dve, ln_act, m["h"][:, :, 0:D], m)


def write_result(nc, ctx, sem, sb, m, out):
    coef = sb("coef", [P, T])
    den, coef_done, ratio, summed, stored = (sem(k) for k in ("den", "coef_done", "ratio", "summed", "stored"))
    q, ac = m["sums"][:, :, 0:D], m["sums"][:, :, D:F2]
    h = m["h"][:, :, 0:D]
    with nc.Block() as block:
        @block.vector
        def _(dve):
            nc.vector.tensor_scalar(ac, ac, 1e-6, None, ALU.add).then_inc(den, 1)
            nc.vector.tensor_scalar(coef[:], m["deg"][:], 0.0, BETA, ALU.is_equal, ALU.max).then_inc(coef_done, 1)
            dve.wait_ge(den, 1)
            nc.vector.reciprocal(ac, ac).then_inc(den, 1)
            dve.wait_ge(coef_done, 1)
            nc.vector.tensor_tensor(h, h, coef[:].unsqueeze(2).to_broadcast([P, T, D]), ALU.mult).then_inc(coef_done, 1)
            dve.wait_ge(den, 2)
            nc.vector.scalar_tensor_tensor(out=q, in0=q, scalar=1.0 - BETA, in1=ac, op0=ALU.mult, op1=ALU.mult).then_inc(ratio, 1)
            dve.wait_ge(coef_done, 2)
            nc.vector.tensor_tensor(h, h, m["xs"][:], ALU.add).then_inc(coef_done, 1)
            dve.wait_ge(ratio, 1)
            dve.wait_ge(coef_done, 3)
            nc.vector.tensor_tensor(m["tmp"][:], h, q, ALU.add).then_inc(summed, 1)

        @block.sync
        def _(sp):
            sp.wait_ge(summed, 1)
            sp.dma_start(out[0:(T - 1) * P, :].rearrange("(t p) f -> p t f", p=P), m["tmp"][:, 0:T - 1, :]).then_inc(stored, 16)
            sp.dma_start(out[(T - 1) * P:N, :], m["tmp"][0:TAIL, T - 1, :]).then_inc(stored, 16)
            sp.wait_ge(stored, 32)


_INS = ['x', 'src', 'dst', 'edge_attr3_2x64', 'L0_gnn_W', 'L0_gnn_b']


def kernel(**inputs):
    import numpy as _np
    import concourse.bacc as _bacc
    from concourse import mybir as _mybir
    from concourse.bass_utils import run_bass_kernel_spmd as _run

    nc = _bacc.Bacc("TRN2", target_bir_lowering=False, num_devices=1)
    arrays, args = {}, []
    for name in _INS:
        a = _np.ascontiguousarray(inputs[name])
        arrays[f"in_{name}_dram"] = a
        args.append(nc.dram_tensor(f"in_{name}_dram", a.shape, _mybir.dt.from_np(a.dtype), kind="ExternalInput").ap())
    out = nc.dram_tensor("out_0_dram", (N, D), F32, kind="ExternalOutput").ap()
    build(nc, *args, out)
    r = _run(nc, [arrays], core_ids=[0])
    return r.results[0]["out_0_dram"]
```

```python
from contextlib import ExitStack

import concourse.bass as bass
from concourse import mybir
from concourse.alu_op_type import AluOpType as ALU

ACT = mybir.ActivationFunctionType
AX = mybir.AxisListType
F32 = mybir.dt.float32
BF16 = mybir.dt.bfloat16
I32 = mybir.dt.int32
U32 = mybir.dt.uint32

P = 128
N = 6250
E = 206250
D = 64
F2 = 2 * D
T = (N + P - 1) // P
NP = T * P
TAIL = N - (T - 1) * P
H1 = D + 1
EPS = 1e-5
BETA = 0.2
GAMMA = 0.95

GC = 125
GN = E // GC
TG = 7
assert GC * GN == E and T % TG == 0

WD = 8
WT = P // WD
WN = T * WT
WV = 3
WE = WV * P
KW = T * WD
KM = 4
KS = 512
WS = 4
OS = 2
BS = 4
WNP = 7 * P
AR, AC = 110, 1875
LR = 375
LN = E // LR
assert AR * AC == E and LN * LR == E and AC % LR == 0 and KW < KS and WN + KM <= WNP

SK = 8
SE = SK * P
SN = (E + SE - 1) // SE
SW = 64
SO = SN * SE - E
ER = 4
H3 = H1 + 2 * D
FP16 = mybir.dt.float16
assert (SN - 2) % ER == 0 and WN % KM == 0


def build(nc, x, src, dst, edge, W, b, out):
    ctx = ExitStack()
    with ctx:
        def sb(name, shape, dt=F32):
            return ctx.enter_context(nc.sbuf_tensor(name, shape, dt))

        def sem(name):
            return ctx.enter_context(nc.semaphore(name))

        mem = dict(
            xs=sb("xs", [P, T, D]), h=sb("h", [P, T, H1]), tmp=sb("tmp", [P, T, D]), stat=sb("stat", [P, 4, T]),
            ident=sb("ident", [P, P]), W=sb("W_sb", [P, D]), bias=sb("bias", [P, D]),
            sums=sb("sums", [P, T, F2]), z=sb("z", [P, T]), deg=sb("deg", [P, T]), eps=sb("eps", [P, 1]))
        for name, shape in (("h_dram", [NP, H1]), ("acc1_dram", [NP, H1]), ("z_dram", [NP, 1]), ("acc2_dram", [NP, F2])):
            mem[name] = nc.dram_tensor(name, shape, F32).ap()
        m = mem
        m["key_dram"] = nc.dram_tensor("key_dram", [E + WE, 2], FP16).ap()
        m["square_dram"] = nc.dram_tensor("square_dram", [3, E], BF16).ap()
        m["bases"] = sb("bases", [1, SN + 2], I32)
        m["basef"] = sb("basef", [1, SN])
        m["src8"] = sb("src8", [P, SN, SK], I32)
        m["dst8"] = sb("dst8", [P, SN, SK], I32)
        m["h3"] = sb("h3", [P, T, H3], BF16)
        m["start_dram"] = nc.dram_tensor("start_dram", [WNP], F32).ap()
        m["starts"] = sb("starts", [1, WNP], I32)
        m["irregular"] = sb("irregular", [1, 1], I32)
        prepare(nc, ctx, sem, mem, x, W, b)
        index_edges(nc, sem, mem, src, dst)
        irregular = nc.values_load(m["irregular"][0:1, 0:1], min_val=0, max_val=8 * P)
        with nc.If(irregular > 0):
            general_sums(nc, sem, mem, src, dst, edge, 1)
        with nc.Else():
            window_sums(nc, sem, mem, src, dst)
        update_nodes(nc, sem, mem)
        with nc.If(irregular > 0):
            general_sums(nc, sem, mem, src, dst, edge, 2)
        with nc.Else():
            block_sums(nc, sem, mem, edge)
        write_result(nc, ctx, sem, sb, mem, out)


def prepare(nc, ctx, sem, m, x, W, b):
    tail_zero, x_in, w_in = sem("tail_zero"), sem("x_in"), sem("w_in")
    id_zero, id_done = sem("id_zero"), sem("id_done")
    xv = x[0:(T - 1) * P, :].rearrange("(t p) f -> p t f", p=P)
    ln_dve, ln_act = sem("ln1_dve"), sem("ln1_act")
    eps_set, ones_set, h_part, h_rest = (sem(k) for k in ("eps_set", "ones_set", "h_part", "h_rest"))
    with nc.Block() as block:
        @block.sync
        def _(sp):
            sp.dma_start(m["xs"][:, 0:T - 1, :], xv).then_inc(x_in, 16)
            sp.wait_ge(tail_zero, 1)
            sp.dma_start(m["xs"][0:TAIL, T - 1, :], x[(T - 1) * P:N, :]).then_inc(x_in, 16)
            sp.dma_start(m["W"][:], W).then_inc(w_in, 16)
            sp.dma_start(m["bias"][:], b.rearrange("(o f) -> o f", o=1).to_broadcast([P, D])).then_inc(w_in, 16)
            sp.wait_ge(w_in, 32)

        @block.gpsimd
        def _(pool):
            nc.gpsimd.memset(m["xs"][:, T - 1, :], 0.0).then_inc(tail_zero, 1)
            nc.gpsimd.memset(m["eps"][:], EPS).then_inc(eps_set, 1)
            nc.gpsimd.memset(m["h"][:, :, D:H1], 1.0).then_inc(ones_set, 1)
            nc.gpsimd.memset(m["ident"][:], 0.0).then_inc(id_zero, 1)
            pool.wait_ge(id_zero, 1)
            nc.gpsimd.affine_select(out=m["ident"][:], in_=m["ident"][:], compare_op=ALU.not_equal, fill=1.0,
                                    base=0, pattern=[[-1, P]], channel_multiplier=1).then_inc(id_done, 1)

        @block.vector
        def _(dve):
            dve.wait_ge(x_in, 32)
            normalize_dve(nc, dve, ln_dve, ln_act, m["xs"][:], m["h"][:, :, 0:D], m)
            dve.wait_ge(h_part, 1)
            nc.vector.tensor_tensor(m["tmp"][:], m["h"][:, :, 0:D], m["h3"][:, :, 0:D], ALU.subtract).then_inc(h_rest, 1)
            dve.wait_ge(h_part, 2)
            nc.vector.tensor_tensor(m["tmp"][:], m["tmp"][:], m["h3"][:, :, H1:H1 + D], ALU.subtract).then_inc(h_rest, 1)

        @block.scalar
        def _(act):
            act.wait_ge(eps_set, 1)
            normalize_act(nc, act, ln_dve, ln_act, m["h"][:, :, 0:D], m)
            act.wait_ge(ln_dve, 6)
            act.wait_ge(ones_set, 1)
            nc.scalar.copy(m["h3"][:, :, 0:H1], m["h"][:]).then_inc(h_part, 1)
            act.wait_ge(h_rest, 1)
            nc.scalar.copy(m["h3"][:, :, H1:H1 + D], m["tmp"][:]).then_inc(h_part, 1)
            act.wait_ge(h_rest, 2)
            nc.scalar.copy(m["h3"][:, :, H1 + D:H3], m["tmp"][:]).then_inc(h_part, 1)


def normalize_dve(nc, dve, ln_dve, ln_act, xin, hout, m):
    mean, ssq, std, rstd = (m["stat"][:, i, :] for i in range(4))
    nc.vector.reduce_sum(ssq, xin, AX.X).then_inc(ln_dve, 1)
    dve.wait_ge(ln_dve, 1)
    nc.vector.tensor_scalar(mean, ssq, 1.0 / D, None, ALU.mult).then_inc(ln_dve, 1)
    dve.wait_ge(ln_dve, 2)
    nc.vector.tensor_tensor(hout, xin, mean.unsqueeze(2).to_broadcast([P, T, D]), ALU.subtract).then_inc(ln_dve, 1)
    dve.wait_ge(ln_act, 1)
    nc.vector.reduce_sum(ssq, m["tmp"][:], AX.X).then_inc(ln_dve, 1)
    dve.wait_ge(ln_act, 2)
    nc.vector.reciprocal(rstd, std).then_inc(ln_dve, 1)
    dve.wait_ge(ln_dve, 5)
    nc.vector.scalar_tensor_tensor(out=hout, in0=hout, scalar=0.0, in1=rstd.unsqueeze(2).to_broadcast([P, T, D]),
                                   op0=ALU.max, op1=ALU.mult).then_inc(ln_dve, 1)


def normalize_act(nc, act, ln_dve, ln_act, hout, m):
    act.wait_ge(ln_dve, 3)
    nc.scalar.activation(m["tmp"][:], hout, ACT.Square).then_inc(ln_act, 1)
    act.wait_ge(ln_dve, 4)
    nc.scalar.activation(m["stat"][:, 2, :], m["stat"][:, 1, :], ACT.Sqrt, bias=m["eps"][:], scale=1.0 / D).then_inc(ln_act, 1)


def general_sums(nc, sem, m, src, dst, edge, layer):
    with ExitStack() as ctx:
        _general_sums(nc, ctx, sem, m, src, dst, edge, layer)


def _general_sums(nc, ctx, sem, m, src, dst, edge, layer):
    R = H1 if layer == 1 else F2
    n = f"g{layer}_"

    def sb(name, shape, dt=F32):
        return ctx.enter_context(nc.sbuf_tensor(name, shape, dt))

    acc = m["acc1_dram"] if layer == 1 else m["acc2_dram"]
    idx = sb(n + "idx", [GC, 2], I32)
    dstf = sb(n + "dstf", [GC, 1])
    same = sb(n + "same", [GC, GC])
    vals = sb(n + "vals", [GC, R])
    old = sb(n + "old", [GC, R])
    new = sb(n + "new", [GC, R])
    zero = sb(n + "zero", [P, R])
    zsrc = sb(n + "zsrc", [GC, 1])
    dst_row = ctx.enter_context(nc.psum_tensor(n + "dst_row", [GC, GC], F32))
    total = ctx.enter_context(nc.psum_tensor(n + "total", [GC, R], F32))
    names = ["zeroed", "table_out", "acc_zeroed", "acc_written", "idx_in", "edge_in", "rows_in", "dst_cast", "row_ready",
             "same_ready", "vals_ready", "scaled", "sum_ready", "new_ready", "sums_in",
             "gather_begun", "scatter_begun"]
    s = {k: sem(n + k) for k in names}
    srcv = src.rearrange("(c o) -> c o", o=1)
    dstv = dst.rearrange("(c o) -> c o", o=1)
    edgev = edge.rearrange("e a f -> e (a f)")
    per_chunk_loads = 32
    rows_per_chunk = 32
    with nc.Block() as block:
        @block.sync
        def _(sp):
            if layer == 1:
                sp.dma_start(m["h_dram"].rearrange("(t p) f -> p t f", p=P), m["h"][:]).then_inc(s["table_out"], 16)
            else:
                sp.dma_start(m["z_dram"].rearrange("(t p) o -> p t o", p=P), m["z"][:].unsqueeze(2), allow_slow_non_contiguous=True).then_inc(s["table_out"], 16)
            sp.wait_ge(s["zeroed"], 1)
            sp.dma_start(acc.rearrange("(t p) f -> p t f", p=P), zero[:].unsqueeze(1).to_broadcast([P, T, R])).then_inc(s["acc_zeroed"], 16)
            sp.wait_ge(s["acc_zeroed"], 16)
            sp.wait_ge(s["table_out"], 16)

            def load(i):
                sp.dma_start(idx[:, 0:1], srcv[bass.ds(i * GC, GC), :]).then_inc(s["idx_in"], 16)
                sp.dma_start(idx[:, 1:2], dstv[bass.ds(i * GC, GC), :]).then_inc(s["idx_in"], 16)
                if layer == 2:
                    sp.dma_start(vals[:], edgev[bass.ds(i * GC, GC), :]).then_inc(s["edge_in"], 16)

            load(0)
            with sp.Fori(1, GN) as i:
                sp.wait_ge(s["acc_written"], 16 * i)
                load(i)
            sp.wait_ge(s["acc_written"], 16 * GN)
            out = m["sums"][:, :, 0:R]
            sp.dma_start(out, acc.rearrange("(t p) f -> p t f", p=P)).then_inc(s["sums_in"], 16)
            sp.wait_ge(s["sums_in"], 16)

        @block.gpsimd
        def _(pool):
            nc.gpsimd.memset(zero[:], 0.0).then_inc(s["zeroed"], 1)
            with pool.Fori(0, GN) as i:
                pool.wait_ge(s["idx_in"], 32 * i + 32)
                pool.sem_inc(s["gather_begun"], 1)
                if layer == 1:
                    pool.indirect_dma_start(vals[:], None, m["h_dram"], bass.IndirectOffsetOnAxis(idx[:, 0:1].bitcast(U32), 0)).then_inc(s["rows_in"], 16)
                else:
                    pool.indirect_dma_start(zsrc[:], None, m["z_dram"], bass.IndirectOffsetOnAxis(idx[:, 0:1].bitcast(U32), 0)).then_inc(s["rows_in"], 16)
                pool.indirect_dma_start(old[:], None, acc, bass.IndirectOffsetOnAxis(idx[:, 1:2].bitcast(U32), 0)).then_inc(s["rows_in"], 16)
                pool.wait_ge(s["new_ready"], i + 1)
                pool.sem_inc(s["scatter_begun"], 1)
                pool.indirect_dma_start(acc, bass.IndirectOffsetOnAxis(idx[:, 1:2].bitcast(U32), 0), new[:], None).then_inc(s["acc_written"], 16)

        @block.vector
        def _(dve):
            with dve.Fori(0, GN) as i:
                dve.wait_ge(s["idx_in"], 32 * i + 32)
                nc.vector.tensor_copy(dstf[:], idx[:, 1:2]).then_inc(s["dst_cast"], 1)
                dve.wait_ge(s["row_ready"], i + 1)
                nc.vector.tensor_scalar(same[:], dst_row[:], dstf[:], None, ALU.is_equal).then_inc(s["same_ready"], 1)
                dve.wait_ge(s["rows_in"], 32 * i + 32)
                if layer == 2:
                    dve.wait_ge(s["edge_in"], 16 * i + 16)
                    nc.vector.scalar_tensor_tensor(out=vals[:, 0:D], in0=vals[:, D:F2], scalar=zsrc[:], in1=vals[:, 0:D],
                                                   op0=ALU.mult, op1=ALU.add).then_inc(s["vals_ready"], 1)
                dve.wait_ge(s["sum_ready"], i + 1)
                nc.vector.tensor_tensor(new[:], total[:], old[:], ALU.add).then_inc(s["new_ready"], 1)

        @block.tensor
        def _(pe):
            with pe.Fori(0, GN) as i:
                pe.wait_ge(s["dst_cast"], i + 1)
                nc.tensor.matmul(dst_row[:], dstf[:].to_broadcast([GC, GC]), m["ident"][0:GC, 0:GC], start=True, stop=True).then_inc(s["row_ready"], 1)
                pe.wait_ge(s["same_ready"], i + 1)
                if layer == 1:
                    pe.wait_ge(s["rows_in"], 32 * i + 32)
                else:
                    pe.wait_ge(s["vals_ready"], i + 1)
                nc.tensor.matmul(total[:], same[:], vals[:], start=True, stop=True).then_inc(s["sum_ready"], 1)


def index_edges(nc, sem, m, src, dst):
    ctx = ExitStack()
    with ctx:
        def sb(name, shape, dt=F32):
            return ctx.enter_context(nc.sbuf_tensor(name, shape, dt))

        srca, dsta = sb("srca", [AR, AC], I32), sb("dsta", [AR, AC], I32)
        hi8, wid, low, part = (sb(k, [AR, AC], I32) for k in ("hi8", "wid", "low", "part"))
        pairs = sb("pairs", [AR, AC, 2], FP16)
        squares = sb("squares", [AR, 3, AC], BF16)
        pad = sb("pad", [P, WE * 2 // P], FP16)
        last8 = sb("last8", [1, SN], I32)
        span = sb("span", [1, SN + 1])
        follow = sb("follow", [AR, 1], I32)
        diff = sb("diff", [AR, AC], BF16)
        bad = sb("bad", [P, 4])
        badsum = sb("badsum", [P, 1])
        ones = sb("ones_col", [P, 1])
        lastrow = sb("lastrow", [AR, AC // LR])
        w8 = sb("w8", [P, 7])
        w8i = sb("w8i", [P, 7], I32)
        junk = sb("junk", [P, 7, LN], BF16)
        row = sb("row", [P, 7])
        rowi = sb("rowi", [P, 7], I32)
        looked = m["sums"][:].rearrange("p t f -> p (t f)")[:, 0:7 * LR].bitcast(I32).rearrange("p (c l) -> p c l", l=LR)
        lookedf = m["tmp"][:].rearrange("p t f -> p (t f)")[:, 0:7 * LR].rearrange("p (c l) -> p c l", l=LR)
        within = sb("within", [P, 7])
        start = sb("start", [P, 7])
        srow = sb("srow", [1, WNP])
        sdiff = sb("sdiff", [1, WNP])
        far, near = sb("far", [1, WN]), sb("near", [1, 1])
        sq, bases_in = sem("a_squares"), sem("a_bases_in")
        ps_last = ctx.enter_context(nc.psum_tensor("ps_last", [P, 8, P], F32))
        ps_bad = ctx.enter_context(nc.psum_tensor("ps_bad", [1, 1], F32))
        idx_in, src_in, follow_in, key_out, start_out, start_in, row_in = (sem(k) for k in ("a_idx_in", "a_src_in", "a_follow_in", "a_key_out", "a_start_out", "a_start_in", "a_row_in"))
        memsets, w8_made, dve, act, last_spread, bad_total, ident_used = (sem(k) for k in ("a_memsets", "a_w8_made", "a_dve", "a_act", "a_last_spread", "a_bad_total", "a_ident"))
        RC = AC // LR
        with nc.Block() as block:
            @block.sync
            def _(sp):
                sp.dma_start(dsta[:], dst.rearrange("(p c) -> p c", c=AC)).then_inc(idx_in, 16)
                sp.wait_ge(memsets, 1)
                sp.dma_start(follow[0:AR - 1, :], dst.rearrange("(p c) -> p c", c=AC)[1:AR, 0:1], allow_slow_non_contiguous=True).then_inc(follow_in, 16)
                sp.dma_start(srca[:], src.rearrange("(p c) -> p c", c=AC)).then_inc(src_in, 16)
                first = dst[0:(SN - 1) * SE].rearrange("(o s k) -> o s k", o=1, k=SE)
                sp.dma_start(m["bases"][:, 2:SN + 1], first[:, :, 0], allow_slow_non_contiguous=True).then_inc(bases_in, 16)
                sp.dma_start(m["bases"][:, SN + 1:SN + 2], dst[E - SE:E - SE + 1].rearrange("(o s) -> o s", o=1)).then_inc(bases_in, 16)
                sp.dma_start(last8[:, 0:SN - 1], first[:, :, SE - 1], allow_slow_non_contiguous=True).then_inc(bases_in, 16)
                sp.dma_start(last8[:, SN - 1:SN], dst[E - 1:E].rearrange("(o s) -> o s", o=1)).then_inc(bases_in, 16)
                sp.wait_ge(memsets, 4)
                sp.dma_start(m["key_dram"][E:E + WE, :].rearrange("(p j) a -> p (j a)", p=P), pad[:]).then_inc(key_out, 16)
                sp.wait_ge(act, 2)
                sp.dma_start(m["key_dram"][0:E, :].rearrange("(p c) a -> p (c a)", c=AC), pairs[:].rearrange("p c a -> p (c a)")).then_inc(key_out, 16)
                sp.wait_ge(act, 4)
                for k in range(3):
                    sp.dma_start(m["square_dram"][k, :].rearrange("(p c) -> p c", c=AC), squares[:, k, :]).then_inc(key_out, 16)
                sp.wait_ge(key_out, 80)

            @block.gpsimd
            def _(pool):
                nc.gpsimd.memset(follow[:], 1 << 20).then_inc(memsets, 1)
                nc.gpsimd.memset(ones[:], 1.0).then_inc(memsets, 1)
                nc.gpsimd.memset(bad[:], 0.0).then_inc(memsets, 1)
                nc.gpsimd.memset(pad[:], -1.0).then_inc(memsets, 1)
                nc.gpsimd.memset(m["bases"][:, 0:2], 0).then_inc(memsets, 1)
                nc.gpsimd.iota(w8i[:], [[P * WD, 7]], base=0, channel_multiplier=WD).then_inc(w8_made, 1)
                pool.wait_ge(dve, 5)
                for c in range(7):
                    pool.indirect_dma_start(looked[:, c, :], None, dst.rearrange("(r c) -> r c", c=LR), bass.IndirectOffsetOnAxis(rowi[:, c:c + 1].bitcast(U32), 0)).then_inc(row_in, 16)
                pool.wait_ge(row_in, 112)

            @block.vector
            def _(v):
                v.wait_ge(idx_in, 16)
                nc.vector.tensor_copy(lastrow[:], dsta[:].rearrange("p (r c) -> p r c", c=LR)[:, :, LR - 1]).then_inc(dve, 1)
                v.wait_ge(w8_made, 1)
                nc.vector.tensor_copy(w8[:], w8i[:]).then_inc(dve, 1)
                v.wait_ge(dve, 2)
                v.wait_ge(last_spread, 1)
                for c in range(7):
                    last = nc.vector.tensor_scalar(junk[:, c, 0:RC * AR].rearrange("p (r c) -> p r c", c=AR), ps_last[:, 0:RC, 0:AR], w8[:, c:c + 1], None, ALU.is_lt, ALU.add, accum_out=row[:, c:c + 1])
                    if c == 6:
                        last.then_inc(dve, 1)
                v.wait_ge(dve, 3)
                nc.vector.tensor_scalar(row[:], row[:], float(LN - 1), None, ALU.min).then_inc(dve, 1)
                v.wait_ge(dve, 4)
                nc.vector.tensor_copy(rowi[:], row[:]).then_inc(dve, 1)
                v.wait_ge(src_in, 16)
                nc.vector.tensor_scalar(wid[:], dsta[:], (KM - 1) * WD, 6, ALU.bitwise_and, ALU.logical_shift_left).then_inc(dve, 1)
                nc.vector.tensor_scalar(hi8[:], srca[:], 7, 3, ALU.logical_shift_right, ALU.logical_shift_left).then_inc(dve, 1)
                nc.vector.tensor_scalar(low[:], srca[:], P - 1, None, ALU.bitwise_and).then_inc(dve, 1)
                v.wait_ge(dve, 6)
                nc.vector.scalar_tensor_tensor(out=part[:], in0=dsta[:], scalar=WD - 1, in1=wid[:], op0=ALU.bitwise_and, op1=ALU.bitwise_or).then_inc(dve, 1)
                v.wait_ge(dve, 9)
                nc.vector.tensor_tensor(part[:], part[:], hi8[:], ALU.bitwise_or).then_inc(dve, 1)
                nc.vector.tensor_tensor(diff[:, 0:AC - 1], dsta[:, 1:AC], dsta[:, 0:AC - 1], ALU.subtract).then_inc(dve, 1)
                v.wait_ge(follow_in, 16)
                nc.vector.tensor_tensor(diff[:, AC - 1:AC], follow[:], dsta[:, AC - 1:AC], ALU.subtract).then_inc(dve, 1)
                v.wait_ge(dve, 12)
                nc.vector.tensor_reduce(badsum[0:AR, :], diff[:], AX.X, ALU.min).then_inc(dve, 1)
                v.wait_ge(dve, 13)
                v.wait_ge(memsets, 3)
                nc.vector.tensor_scalar(bad[0:AR, 0:1], badsum[0:AR, :], 0.0, None, ALU.is_lt).then_inc(dve, 1)
                v.wait_ge(row_in, 112)
                nc.vector.tensor_copy(lookedf, looked).then_inc(dve, 1)
                v.wait_ge(dve, 15)
                for c in range(7):
                    last = nc.vector.tensor_scalar(junk[:, c, 0:LR], lookedf[:, c, :], w8[:, c:c + 1], None, ALU.is_lt, ALU.add, accum_out=within[:, c:c + 1])
                    if c == 6:
                        last.then_inc(dve, 1)
                v.wait_ge(dve, 16)
                nc.vector.scalar_tensor_tensor(out=start[:], in0=row[:], scalar=float(LR), in1=within[:], op0=ALU.mult, op1=ALU.add).then_inc(dve, 1)
                nc.vector.tensor_tensor(wid[:], low[:], low[:], ALU.mult).then_inc(sq, 1)
                v.wait_ge(sq, 1)
                nc.vector.tensor_scalar(hi8[:], wid[:], 0x3F00, None, ALU.bitwise_and).then_inc(sq, 1)
                nc.vector.tensor_scalar(wid[:], wid[:], 0xFF, None, ALU.bitwise_and).then_inc(sq, 1)
                v.wait_ge(bases_in, 64)
                v.wait_ge(memsets, 5)
                nc.vector.tensor_tensor(span[:, 0:SN], last8[:], m["bases"][:, 2:SN + 2], ALU.subtract).then_inc(sq, 1)
                v.wait_ge(sq, 4)
                nc.vector.tensor_reduce(span[:, SN:SN + 1], span[:, 0:SN], AX.X, ALU.max).then_inc(sq, 1)
                nc.vector.tensor_scalar(m["bases"][:], m["bases"][:], NP - SW, None, ALU.min).then_inc(sq, 1)
                v.wait_ge(sq, 6)
                nc.vector.tensor_scalar(bad[0:1, 2:3], span[:, SN:SN + 1], float(SW - 1), None, ALU.is_gt).then_inc(sq, 1)
                nc.vector.tensor_copy(m["basef"][:], m["bases"][:, 2:SN + 2]).then_inc(sq, 1)
                v.wait_ge(start_in, 16)
                nc.vector.tensor_tensor(sdiff[:, 0:WN], srow[:, 1:WN + 1], srow[:, 0:WN], ALU.subtract).then_inc(dve, 1)
                v.wait_ge(dve, 18)
                nc.vector.tensor_reduce(sdiff[:, WN:WN + 1], sdiff[:, 0:WN], AX.X, ALU.max).then_inc(dve, 1)
                v.wait_ge(dve, 19)
                nc.vector.tensor_scalar(bad[0:1, 1:2], sdiff[:, WN:WN + 1], float(WE), None, ALU.is_gt).then_inc(dve, 1)
                nc.vector.tensor_copy(m["starts"][:], srow[:]).then_inc(dve, 1)
                nc.vector.tensor_scalar(far[:], srow[:, KM:WN + KM], float(E), float(WE), ALU.is_ge, ALU.mult).then_inc(dve, 1)
                v.wait_ge(dve, 22)
                nc.vector.tensor_tensor(far[:], far[:], srow[:, KM:WN + KM], ALU.add).then_inc(dve, 1)
                v.wait_ge(dve, 23)
                nc.vector.tensor_tensor(far[:], far[:], srow[:, 0:WN], ALU.subtract).then_inc(dve, 1)
                v.wait_ge(dve, 24)
                nc.vector.tensor_reduce(near[:], far[:], AX.X, ALU.min).then_inc(dve, 1)
                v.wait_ge(dve, 25)
                nc.vector.tensor_scalar(bad[0:1, 3:4], near[:], float(WE), None, ALU.is_lt).then_inc(dve, 1)
                v.wait_ge(dve, 26)
                v.wait_ge(sq, 7)
                nc.vector.reduce_sum(badsum[:], bad[:], AX.X).then_inc(dve, 1)
                v.wait_ge(bad_total, 1)
                nc.vector.tensor_copy(m["irregular"][:], ps_bad[:]).then_inc(dve, 1)

            @block.tensor
            def _(pe):
                pe.wait_ge(dve, 1)
                for r in range(RC):
                    last = nc.tensor.matmul(ps_last[:, r, 0:AR], lastrow[:, r:r + 1].to_broadcast([AR, P]), m["ident"][0:AR, 0:AR], start=True, stop=True)
                last.then_inc(last_spread, 1)
                pe.wait_ge(dve, 27)
                nc.tensor.matmul(ps_bad[:], badsum[:], ones[:], start=True, stop=True).then_inc(bad_total, 1)

            @block.scalar
            def _(a):
                a.wait_ge(dve, 8)
                nc.scalar.copy(squares[:, 0, :], low[:])
                nc.scalar.copy(pairs[:, :, 1], low[:]).then_inc(act, 1)
                a.wait_ge(dve, 10)
                nc.scalar.copy(pairs[:, :, 0], part[:]).then_inc(act, 1)
                a.wait_ge(sq, 3)
                nc.scalar.copy(squares[:, 1, :], hi8[:]).then_inc(act, 1)
                nc.scalar.copy(squares[:, 2, :], wid[:]).then_inc(act, 1)
                a.wait_ge(dve, 17)
                a.dma_start(m["start_dram"].rearrange("(c p) -> p c", p=P), start[:], allow_slow_non_contiguous=True).then_inc(start_out, 16)
                a.wait_ge(start_out, 16)
                a.dma_start(srow[:], m["start_dram"].rearrange("(o c) -> o c", o=1)).then_inc(start_in, 16)


def window_sums(nc, sem, m, src, dst):
    ctx = ExitStack()
    with ctx:
        def sb(name, shape, dt=F32):
            return ctx.enter_context(nc.sbuf_tensor(name, shape, dt))

        iota_i = sb("iota_i", [P, KW], I32)
        iota = sb("iota", [P, KW], FP16)
        keys = sb("keys", [P, WS, WV, 2], FP16)
        hot_src = sb("hot_src", [P, OS, WV, P], BF16)
        hot_key = sb("hot_key", [P, OS, WV, KW], BF16)
        counts = sb("counts", [P, 2, T, P], FP16)
        parts = sb("parts", [P, T, H3])
        ps_counts = [ctx.enter_context(nc.psum_tensor(f"ps_counts{k}", [P, 512], F32)) for k in range(BS)]
        ps_sums = [ctx.enter_context(nc.psum_tensor(f"ps_sums{k}", [P, 512], F32)) for k in range(2)]
        iotas, iota_cast, dve_parts, edges_in = sem("w_iotas"), sem("w_iota_cast"), sem("w_dve_parts"), sem("w_edges_in")
        keys_in = [sem(f"w_keys_in{k}") for k in range(WS)]
        hots_made, counted, counts_out, summed, sums_out = (sem(k) for k in ("w_hots_made", "w_counted", "w_counts_out", "w_summed", "w_sums_out"))
        with nc.Block() as block:
            @block.sync
            def _(sp):
                sp.sem_inc(hots_made, WS)
                with sp.Fori(0, WN, WS) as g:
                    _, starts = nc.values_load_multi_w_load_instructions(
                        m["starts"][0:1, bass.ds(g, WS)], engines=[mybir.EngineType.SP], min_val=0, max_val=E,
                        skip_runtime_bounds_check_because="a start counts edges, of which there are E")
                    for k in range(WS):
                        sp.wait_ge(hots_made, g + k + 1)
                        sp.dma_start(keys[:, k, :, :].rearrange("p j a -> p (j a)"),
                                     m["key_dram"][bass.ds(starts[k], WE), :].rearrange("(p j) a -> p (j a)", j=WV)).then_inc(keys_in[k], 16)

            @block.gpsimd
            def _(pool):
                nc.gpsimd.iota(iota_i[:], [[1, KW]], base=0, channel_multiplier=0).then_inc(iotas, 1)

            @block.vector
            def _(dve):
                dve.sem_inc(counted, OS)
                dve.wait_ge(iotas, 1)
                nc.vector.tensor_copy(iota[:], iota_i[:]).then_inc(iota_cast, 1)
                dve.wait_ge(iota_cast, 1)
                with dve.Fori(0, T) as t:
                    for i in range(WT):
                        k = i % WS
                        dve.wait_ge(keys_in[k], t * (WT // WS * 16) + (i // WS + 1) * 16)
                        dve.wait_ge(counted, t * WT + (i + 1))
                        for j in range(WV):
                            nc.vector.tensor_scalar(hot_src[:, i % OS, j, :], iota[:, 0:P], keys[:, k, j, 1:2], None, ALU.is_equal)
                            last = nc.vector.tensor_scalar(hot_key[:, i % OS, j, :], iota[:], float(i % KM * KS), keys[:, k, j, 0:1], ALU.add, ALU.is_equal)
                        last.then_inc(hots_made, 1)
                dve.wait_ge(sums_out, T + 2)
                nc.vector.tensor_tensor(parts[:, :, H1:H1 + D], parts[:, :, H1:H1 + D], parts[:, :, H1 + D:H3], ALU.add).then_inc(dve_parts, 1)
                nc.vector.tensor_copy(m["sums"][:, :, D:H1], parts[:, :, D:H1])
                dve.wait_ge(dve_parts, 1)
                nc.vector.tensor_tensor(m["sums"][:, :, 0:D], parts[:, :, 0:D], parts[:, :, H1:H1 + D], ALU.add)

            @block.tensor
            def _(pe):
                pe.sem_inc(counts_out, BS)
                pe.sem_inc(sums_out, 2)

                def product(t, half):
                    pe.wait_ge(counts_out, t * WT + (WT + BS))
                    pe.wait_ge(sums_out, t + 1)
                    for c in range(T):
                        last = nc.tensor.matmul(ps_sums[half][:, 0:H3], counts[:, half, c, :], m["h3"][:, c, :], start=(c == 0), stop=(c == T - 1))
                    last.then_inc(summed, 1)

                def count(t, half, first=False):
                    for i in range(WT):
                        pe.wait_ge(hots_made, t * WT + (i + 1 + WS))
                        pe.wait_ge(counts_out, t * WT + (i + 1))
                        for j in range(WV):
                            last = nc.tensor.matmul(ps_counts[i % BS][:, 0:KW], hot_src[:, i % OS, j, :], hot_key[:, i % OS, j, :], start=(j == 0), stop=(j == WV - 1))
                        last.then_inc(counted, 1)
                        if i == 1 and not first:
                            product(t - 1, 1 - half)

                count(0, 0, first=True)
                with pe.Fori(1, T, 2) as t:
                    count(t, 1)
                    count(t + 1, 0)
                product(T - 1, 0)

            @block.scalar
            def _(act):
                act.sem_inc(summed, 2)
                for t8, v in ((m["dst8"], dst), (m["src8"], src)):
                    act.dma_start(t8[:, 0:SN - 1, :], v[0:(SN - 1) * SE].rearrange("(s p j) -> p s j", p=P, j=SK)).then_inc(edges_in, 16)
                    act.dma_start(t8[:, SN - 1, :], v[E - SE:E].rearrange("(p j) -> p j", j=SK)).then_inc(edges_in, 16)

                def sums_to_sbuf(t, half):
                    act.wait_ge(summed, t + 3)
                    nc.scalar.copy(parts[:, bass.ds(t, 1), :], ps_sums[half][:, 0:H3].unsqueeze(1)).then_inc(sums_out, 1)

                def counts_to_sbuf(t, half, first=False):
                    act.wait_ge(summed, t + 1)
                    for i in range(WT):
                        act.wait_ge(counted, t * WT + (i + 1 + OS))
                        nc.scalar.copy(counts[:, half, :, i * WD:(i + 1) * WD], ps_counts[i % BS][:, 0:KW].rearrange("p (c d) -> p c d", d=WD)).then_inc(counts_out, 1)
                        if i == 1 and not first:
                            sums_to_sbuf(t - 1, 1 - half)

                counts_to_sbuf(0, 0, first=True)
                with act.Fori(1, T, 2) as t:
                    counts_to_sbuf(t, 1)
                    counts_to_sbuf(t + 1, 0)
                sums_to_sbuf(T - 1, 0)
                act.wait_ge(edges_in, 64)


def block_sums(nc, sem, m, edge):
    with ExitStack() as ctx:
        def sb(name, shape, dt=F32):
            return ctx.enter_context(nc.sbuf_tensor(name, shape, dt))

        def ps(name):
            return ctx.enter_context(nc.psum_tensor(name, [P, 512], F32))

        acc = sb("acc", [P, NP])
        et = sb("et", [P, ER, SK, F2])
        square = sb("square", [3, ER, SE], BF16)
        lhs3 = sb("lhs3", [3, P], BF16)
        two_i = sb("two_i", [1, P], I32)
        part_i = sb("part_i", [P, 1], I32)
        part_f, bias1 = sb("part_f", [P, 1]), sb("bias1", [P, 1])
        iota_i = sb("iota64_i", [P, SW], I32)
        iota = sb("iota64", [P, SW])
        ones1 = sb("ones1", [1, P])
        rel = sb("rel", [P, SN, SK])
        tile_of = sb("tile_of", [P, SN, SK])
        zpart = sb("zpart", [P, 3, T], BF16)
        zrest = sb("zrest", [P, 2, T])
        hot_lo = sb("hot_lo", [P, 2, SE], BF16)
        hot_dst = sb("hot_dst", [P, 2, SK, SW])
        mask = sb("mask", [P, 2, SK, T])
        picked = sb("picked", [P, 2, SK, T])
        zsrc = sb("zsrc", [P, 2, SK])
        ze = sb("ze", [P, 2, SK, D])
        ps_square = [[ps(f"ps_square{i}{k}") for k in range(2)] for i in range(2)]
        ps_z = [ps(f"ps_z{i}") for i in range(2)]
        ps_acc = [ps(f"ps_acc{i}") for i in range(2)]
        consts, setup, base_spread, rel_made, rel_masked = (sem("b_" + k) for k in ("consts", "setup", "base_spread", "rel_made", "rel_masked"))
        rest = sem("b_rest")
        edges_in = [sem(f"b_edges_in{k}") for k in range(ER)]
        squares_in = [sem(f"b_squares_in{k}") for k in range(ER)]
        squared, mask_made, picked_made, z_ready, hots_made = (sem("b_" + k) for k in ("squared", "mask_made", "picked_made", "z_ready", "hots_made"))
        ze_made = sem("b_ze_made")
        lo_made, z_spread, q_made, summed, acc_added = (sem("b_" + k) for k in ("lo_made", "z_spread", "q_made", "summed", "acc_added"))
        rows = edge.rearrange("e a f -> e (a f)")

        def first_edge(s):
            return E - SE if isinstance(s, int) and s == SN - 1 else s * SE

        def blocks(eng, step, lag_before, lag_after):
            for s in range(-lag_before, ER):
                step(s, s % ER)
            with eng.Fori(ER, SN - 1 - ER, ER) as s0:
                for r in range(ER):
                    step(s0 + r, r)
            for s in range(SN - 2, SN + lag_after):
                step(s, s % ER)

        def within(s):
            return not isinstance(s, int) or 0 <= s < SN

        with nc.Block() as block:
            @block.sync
            def _(sp):
                sp.sem_inc(summed, ER)

                def load(s, r):
                    sp.wait_ge(summed, s + 1)
                    sp.dma_start(square[:, r, :], m["square_dram"][:, bass.ds(first_edge(s), SE)]).then_inc(squares_in[r], 16)
                    sp.dma_start(et[:, r, :, :].rearrange("p j f -> p (j f)"),
                                 rows[bass.ds(first_edge(s), SE), :].rearrange("(p j) f -> p (j f)", j=SK)).then_inc(edges_in[r], 16)

                blocks(sp, load, 0, 0)

            @block.tensor
            def _(pe):
                pe.sem_inc(lo_made, 2)
                pe.sem_inc(q_made, 2)
                pe.sem_inc(acc_added, 2)
                pe.wait_ge(consts, 5)
                nc.tensor.matmul(ps_acc[0][:, 0:SN], ones1[:], m["basef"][:], start=True, stop=True).then_inc(base_spread, 1)
                pe.wait_ge(setup, 8)
                pe.wait_ge(rel_made, 1)

                def spread_squares(s, r):
                    pe.wait_ge(squares_in[r], (s - r) * (16 // ER) + 16)
                    pe.wait_ge(lo_made, s + 1)
                    for k in range(2):
                        last = nc.tensor.matmul(ps_square[r % 2][k][:], lhs3[:], square[:, r, k * 512:(k + 1) * 512], start=True, stop=True)
                    last.then_inc(squared, 1)

                def spread_z(s, r):
                    pe.wait_ge(lo_made, s + 3)
                    pe.wait_ge(picked_made, s + 1)
                    for j in range(SK):
                        for k in range(3):
                            last = nc.tensor.matmul(ps_z[r % 2][:, j * T:(j + 1) * T], hot_lo[:, r % 2, j:SE:SK], zpart[:, k, :], start=(k == 0), stop=(k == 2))
                    last.then_inc(z_spread, 1)

                def sum_block(s, r):
                    pe.wait_ge(q_made, s + 3)
                    pe.wait_ge(hots_made, s + 1)
                    pe.wait_ge(acc_added, s + 1)
                    for j in range(SK):
                        last = nc.tensor.matmul(ps_acc[r % 2][:, 0:SW], et[:, r, j, :], hot_dst[:, r % 2, j, :], start=(j == 0), stop=(j == SK - 1))
                    last.then_inc(summed, 1)

                def step(s, r):
                    if within(s + 2 if isinstance(s, int) else s):
                        spread_squares(s + 2, (r + 2) % ER)
                    if within(s + 1 if isinstance(s, int) else s):
                        spread_z(s + 1, (r + 1) % ER)
                    if within(s - 1 if isinstance(s, int) else s):
                        sum_block(s - 1, (r - 1) % ER)

                blocks(pe, step, 2, 1)

            @block.scalar
            def _(act):
                act.sem_inc(z_spread, 2)
                act.wait_ge(setup, 8)

                def one_hot(s, r):
                    act.wait_ge(squared, s + 1)
                    act.wait_ge(z_spread, s + 1)
                    for k in range(2):
                        last = nc.scalar.activation(hot_lo[:, r % 2, k * 512:(k + 1) * 512], ps_square[r % 2][k][:], ACT.Relu, bias=bias1[:])
                    last.then_inc(lo_made, 1)

                blocks(act, one_hot, 0, 0)

            @block.vector
            def _(dve):
                dve.sem_inc(picked_made, 2)
                dve.wait_ge(consts, 5)
                nc.vector.tensor_copy(lhs3[0:1, :], two_i[:]).then_inc(setup, 1)
                nc.vector.tensor_copy(part_f[:], part_i[:]).then_inc(setup, 1)
                nc.vector.tensor_copy(iota[:], iota_i[:]).then_inc(setup, 1)
                nc.vector.tensor_copy(zpart[:, 0, :], m["z"][:]).then_inc(setup, 1)
                dve.wait_ge(setup, 4)
                nc.vector.tensor_tensor(zrest[:, 0, :], m["z"][:], zpart[:, 0, :], ALU.subtract).then_inc(setup, 1)
                nc.vector.tensor_tensor(bias1[:], part_f[:], part_f[:], ALU.mult).then_inc(setup, 1)
                dve.wait_ge(setup, 6)
                nc.vector.tensor_scalar(bias1[:], bias1[:], -1.0, 1.0, ALU.mult, ALU.add).then_inc(setup, 1)
                nc.vector.tensor_copy(zpart[:, 1, :], zrest[:, 0, :]).then_inc(rest, 1)
                dve.wait_ge(rest, 1)
                nc.vector.tensor_tensor(zrest[:, 1, :], zrest[:, 0, :], zpart[:, 1, :], ALU.subtract).then_inc(rest, 1)
                dve.wait_ge(rest, 2)
                nc.vector.tensor_copy(zpart[:, 2, :], zrest[:, 1, :]).then_inc(setup, 1)
                dve.wait_ge(base_spread, 1)
                nc.vector.tensor_tensor(rel[:], m["dst8"][:], ps_acc[0][:, 0:SN].unsqueeze(2).to_broadcast([P, SN, SK]), ALU.subtract).then_inc(rel_made, 1)
                nc.vector.tensor_scalar(m["src8"][:], m["src8"][:], 7, None, ALU.logical_shift_right).then_inc(rest, 1)
                dve.wait_ge(rest, 3)
                nc.vector.tensor_copy(tile_of[:], m["src8"][:]).then_inc(rest, 1)
                nc.vector.memset(acc[:], 0.0).then_inc(rest, 1)
                dve.wait_ge(rest, 5)
                dve.wait_ge(rel_masked, 1)

                def pick_z(s, r):
                    h = r % 2
                    nc.vector.tensor_tensor(mask[:, h, :, :], iota[:, 0:T].unsqueeze(1).to_broadcast([P, SK, T]), tile_of[:, bass.ds(s, 1), :].rearrange("p o j -> p (o j)").unsqueeze(2).to_broadcast([P, SK, T]), ALU.is_equal).then_inc(mask_made, 1)
                    dve.wait_ge(mask_made, s + 1)
                    dve.wait_ge(z_spread, s + 3)
                    nc.vector.tensor_tensor(picked[:, h, :, :], mask[:, h, :, :], ps_z[h][:, 0:SK * T].rearrange("p (j t) -> p j t", t=T), ALU.mult).then_inc(picked_made, 1)
                    dve.wait_ge(picked_made, s + 3)
                    dve.wait_ge(q_made, s + 1)
                    nc.vector.reduce_sum(zsrc[:, h, :], picked[:, h, :, :], AX.X).then_inc(z_ready, 1)

                def hot_dsts(s, r):
                    dve.wait_ge(summed, s + 3)
                    nc.vector.tensor_tensor(hot_dst[:, r % 2, :, :], iota[:].unsqueeze(1).to_broadcast([P, SK, SW]), rel[:, bass.ds(s, 1), :].rearrange("p o j -> p (o j)").unsqueeze(2).to_broadcast([P, SK, SW]), ALU.is_equal).then_inc(hots_made, 1)

                def add_block(s, r, base):
                    dve.wait_ge(summed, s + 5)
                    dve.wait_ge(acc_added, s + 2)
                    at = acc[:, bass.ds(base, SW)]
                    nc.vector.tensor_tensor(at, at, ps_acc[r % 2][:, 0:SW], ALU.add).then_inc(acc_added, 1)

                def step(s, r, base):
                    if within(s):
                        pick_z(s, r)
                    if within(s - 1 if isinstance(s, int) else s):
                        hot_dsts(s - 1, (r - 1) % ER)
                    if within(s - 2 if isinstance(s, int) else s):
                        add_block(s - 2, (r - 2) % ER, base)

                def base_of(s, n):
                    return nc.values_load_multi_w_load_instructions(
                        m["bases"][0:1, bass.ds(s, n)], engines=[mybir.EngineType.DVE], min_val=0, max_val=NP - SW,
                        skip_runtime_bounds_check_because="the bases are clamped to this range when they are computed")[1]

                for s in range(ER):
                    step(s, s % ER, base_of(s, 1)[0] if s >= 2 else None)
                with dve.Fori(ER, SN - 1 - ER, ER) as s0:
                    base = base_of(s0, ER)
                    for r in range(ER):
                        step(s0 + r, r, base[r])
                for s in range(SN - 2, SN + 2):
                    step(s, s % ER, base_of(s, 1)[0])

            @block.gpsimd
            def _(pool):
                nc.gpsimd.memset(lhs3[:], -1.0).then_inc(consts, 1)
                nc.gpsimd.iota(two_i[:], [[2, P]], base=0, channel_multiplier=0).then_inc(consts, 1)
                nc.gpsimd.iota(part_i[:], [[0, 1]], base=0, channel_multiplier=1).then_inc(consts, 1)
                nc.gpsimd.iota(iota_i[:], [[1, SW]], base=0, channel_multiplier=0).then_inc(consts, 1)
                nc.gpsimd.memset(ones1[:], 1.0).then_inc(consts, 1)
                pool.wait_ge(rel_made, 1)
                nc.gpsimd.affine_select(out=rel[:, SN - 1, :], in_=rel[:, SN - 1, :], compare_op=ALU.is_ge, fill=-1.0,
                                        base=-SO, pattern=[[1, SK]], channel_multiplier=SK).then_inc(rel_masked, 1)

                def scale(s, r):
                    pool.wait_ge(edges_in[r], (s - r) * (16 // ER) + 16)
                    pool.wait_ge(z_ready, s + 1)
                    e0, e1 = et[:, r, :, 0:D], et[:, r, :, D:F2]
                    nc.gpsimd.tensor_tensor(ze[:, r % 2, :, :], e1, zsrc[:, r % 2, :].unsqueeze(2).to_broadcast([P, SK, D]), ALU.mult).then_inc(ze_made, 1)
                    pool.wait_ge(ze_made, s + 1)
                    nc.gpsimd.tensor_tensor(e0, e0, ze[:, r % 2, :, :], ALU.add).then_inc(q_made, 1)

                blocks(pool, scale, 0, 0)

        turned, sums_out = sem("b_turned"), sem("b_sums_out")
        banks = [b for pair in ps_square for b in pair] + ps_z + ps_acc
        with nc.Block() as block:
            @block.tensor
            def _(pe):
                for t in range(T):
                    if t // 4 >= 8 and t % 4 == 0:
                        pe.wait_ge(sums_out, t // 4 - 7)
                    last = nc.tensor.transpose(banks[t // 4 % 8][:, t % 4 * P:(t % 4 + 1) * P], acc[:, t * P:(t + 1) * P], m["ident"][:])
                    if t % 4 == 3 or t == T - 1:
                        last.then_inc(turned, 1)

            @block.vector
            def _(dve):
                for g in range((T + 3) // 4):
                    n = min(4, T - 4 * g)
                    dve.wait_ge(turned, g + 1)
                    nc.vector.tensor_copy(m["sums"][:, 4 * g:4 * g + n, :], banks[g % 8][:, 0:n * P].rearrange("p (t f) -> p t f", f=P)).then_inc(sums_out, 1)


def update_nodes(nc, sem, m):
    with ExitStack() as ctx:
        _update_nodes(nc, ctx, sem, m)


def _update_nodes(nc, ctx, sem, m):
    def sb(name, shape, dt=F32):
        return ctx.enter_context(nc.sbuf_tensor(name, shape, dt))

    cat = sb("cat", [P, TG, F2])
    catT = sb("catT", [P, TG, P])
    rdeg = sb("rdeg", [P, T])
    psT = ctx.enter_context(nc.psum_tensor("psT", [P, 8, P], F32))
    psY = ctx.enter_context(nc.psum_tensor("psY", [P, 8, D], F32))
    deg_done, rdeg_done, bias_added, h_copied, n_scaled = (sem(k) for k in ("deg_done", "rdeg_done", "bias_added", "h_copied", "n_scaled"))
    turned, turned_out, projected, x_updated = (sem(k) for k in ("turned", "turned_out", "projected", "x_updated"))
    ln_dve, ln_act, z_max = sem("ln2_dve"), sem("ln2_act"), sem("z_max")
    with nc.Block() as block:
        @block.vector
        def _(dve):
            nc.vector.tensor_copy(m["deg"][:].unsqueeze(2), m["sums"][:, :, D:H1]).then_inc(deg_done, 1)
            dve.wait_ge(deg_done, 1)
            nc.vector.tensor_scalar(rdeg[:], m["deg"][:], 1.0, None, ALU.max).then_inc(rdeg_done, 1)
            dve.wait_ge(rdeg_done, 1)
            nc.vector.reciprocal(rdeg[:], rdeg[:]).then_inc(rdeg_done, 1)
            nc.vector.tensor_tensor(m["xs"][:], m["xs"][:], m["bias"][:].unsqueeze(1).to_broadcast([P, T, D]), ALU.add).then_inc(bias_added, 1)
            dve.wait_ge(rdeg_done, 2)
            nc.vector.tensor_tensor(m["sums"][:, :, 0:D], m["sums"][:, :, 0:D], rdeg[:].unsqueeze(2).to_broadcast([P, T, D]), ALU.mult).then_inc(n_scaled, 1)
            dve.wait_ge(bias_added, 1)
            dve.wait_ge(n_scaled, 1)
            with dve.Fori(0, T // TG) as g:
                nc.vector.tensor_copy(cat[:, :, 0:D], m["h"][:, bass.ds(g * TG, TG), 0:D]).then_inc(h_copied, 1)
                nc.vector.tensor_copy(cat[:, :, D:F2], m["sums"][:, bass.ds(g * TG, TG), 0:D]).then_inc(h_copied, 1)
                dve.wait_ge(projected, g + 1)
                xg = m["xs"][:, bass.ds(g * TG, TG), :]
                nc.vector.tensor_tensor(xg, xg, psY[:, 0:TG, :], ALU.add).then_inc(x_updated, 1)
            dve.wait_ge(x_updated, T // TG)
            normalize_dve(nc, dve, ln_dve, ln_act, m["xs"][:], m["h"][:, :, 0:D], m)
            dve.wait_ge(ln_dve, 6)
            nc.vector.tensor_reduce(m["z"][:], m["h"][:, :, 0:D], AX.X, ALU.max).then_inc(z_max, 1)
            dve.wait_ge(z_max, 1)
            nc.vector.tensor_scalar(m["z"][:], m["z"][:], GAMMA, None, ALU.mult).then_inc(z_max, 1)

        @block.tensor
        def _(pe):
            with pe.Fori(0, T // TG) as g:
                pe.wait_ge(h_copied, 2 * g + 2)
                for k in range(TG):
                    last = nc.tensor.transpose(psT[:, k, :], cat[:, k, :], m["ident"][:])
                last.then_inc(turned, 1)
                pe.wait_ge(turned_out, g + 1)
                for k in range(TG):
                    last = nc.tensor.matmul(psY[:, k, :], catT[:, k, :], m["W"][:], start=True, stop=True)
                last.then_inc(projected, 1)

        @block.scalar
        def _(act):
            with act.Fori(0, T // TG) as g:
                act.wait_ge(turned, g + 1)
                nc.scalar.copy(catT[:], psT[:, 0:TG, :]).then_inc(turned_out, 1)
            normalize_act(nc, act, ln_dve, ln_act, m["h"][:, :, 0:D], m)


def write_result(nc, ctx, sem, sb, m, out):
    coef = sb("coef", [P, T])
    den, coef_done, ratio, summed, stored = (sem(k) for k in ("den", "coef_done", "ratio", "summed", "stored"))
    q, ac = m["sums"][:, :, 0:D], m["sums"][:, :, D:F2]
    h = m["h"][:, :, 0:D]
    with nc.Block() as block:
        @block.vector
        def _(dve):
            nc.vector.tensor_scalar(ac, ac, 1e-6, None, ALU.add).then_inc(den, 1)
            nc.vector.tensor_scalar(coef[:], m["deg"][:], 0.0, BETA, ALU.is_equal, ALU.max).then_inc(coef_done, 1)
            dve.wait_ge(den, 1)
            nc.vector.reciprocal(ac, ac).then_inc(den, 1)
            dve.wait_ge(coef_done, 1)
            nc.vector.tensor_tensor(h, h, coef[:].unsqueeze(2).to_broadcast([P, T, D]), ALU.mult).then_inc(coef_done, 1)
            dve.wait_ge(den, 2)
            nc.vector.scalar_tensor_tensor(out=q, in0=q, scalar=1.0 - BETA, in1=ac, op0=ALU.mult, op1=ALU.mult).then_inc(ratio, 1)
            dve.wait_ge(coef_done, 2)
            nc.vector.tensor_tensor(h, h, m["xs"][:], ALU.add).then_inc(coef_done, 1)
            dve.wait_ge(ratio, 1)
            dve.wait_ge(coef_done, 3)
            nc.vector.tensor_tensor(m["tmp"][:], h, q, ALU.add).then_inc(summed, 1)

        @block.sync
        def _(sp):
            sp.wait_ge(summed, 1)
            sp.dma_start(out[0:(T - 1) * P, :].rearrange("(t p) f -> p t f", p=P), m["tmp"][:, 0:T - 1, :]).then_inc(stored, 16)
            sp.dma_start(out[(T - 1) * P:N, :], m["tmp"][0:TAIL, T - 1, :]).then_inc(stored, 16)
            sp.wait_ge(stored, 32)


_INS = ['x', 'src', 'dst', 'edge_attr3_2x64', 'L0_gnn_W', 'L0_gnn_b']


def kernel(**inputs):
    import numpy as _np
    import concourse.bacc as _bacc
    from concourse import mybir as _mybir
    from concourse.bass_utils import run_bass_kernel_spmd as _run

    nc = _bacc.Bacc("TRN2", target_bir_lowering=False, num_devices=1)
    arrays, args = {}, []
    for name in _INS:
        a = _np.ascontiguousarray(inputs[name])
        arrays[f"in_{name}_dram"] = a
        args.append(nc.dram_tensor(f"in_{name}_dram", a.shape, _mybir.dt.from_np(a.dtype), kind="ExternalInput").ap())
    out = nc.dram_tensor("out_0_dram", (N, D), F32, kind="ExternalOutput").ap()
    build(nc, *args, out)
    r = _run(nc, [arrays], core_ids=[0])
    return r.results[0]["out_0_dram"]
```

```python
from contextlib import ExitStack

import concourse.bass as bass
from concourse import mybir
from concourse.alu_op_type import AluOpType as ALU

ACT = mybir.ActivationFunctionType
AX = mybir.AxisListType
F32 = mybir.dt.float32
BF16 = mybir.dt.bfloat16
FP16 = mybir.dt.float16
I32 = mybir.dt.int32
U32 = mybir.dt.uint32

P = 128
N = 6250
E = 206250
D = 64
F2 = 2 * D
T = (N + P - 1) // P
NP = T * P
TAIL = N - (T - 1) * P
H1 = D + 1
H3 = 2 * H1 + D
EPS = 1e-5
BETA = 0.2
GAMMA = 0.95

GC = 125
GN = E // GC
TG = 7
assert GC * GN == E and T % TG == 0

WD = 8
WT = P // WD
WN = T * WT
WV = 3
WE = WV * P
KW = T * WD
KM = 4
KS = 512
WS = 8
OS = 4
BS = 2
WK = 4 * WV + 2

QG = 4
GD = P // QG
GV = 10
GE = GV * P
GT = 9
NG = GT * QG
NW = T - GT
assert NG == NW - 4 and GV <= WT

WNP = 7 * P
AR, AC = 110, 1875
LR = 375
LN = E // LR
assert AR * AC == E and LN * LR == E and AC % LR == 0 and KW < KS and WN + KM <= WNP

SK = 8
SE = SK * P
SN = (E + SE - 1) // SE
SW = 64
SO = SN * SE - E
ER = 8
EH = 4
assert (SN - 2) % ER == 0 and WN % KM == 0


def build(nc, x, src, dst, edge, W, b, out):
    ctx = ExitStack()
    with ctx:
        def sb(name, shape, dt=F32):
            return ctx.enter_context(nc.sbuf_tensor(name, shape, dt))

        def sem(name):
            return ctx.enter_context(nc.semaphore(name))

        def shared(sems):
            left = iter(range(1 << 10))

            def take(name):
                k = next(left)
                if k == len(sems):
                    sems.append(sem(f"{name}_{k}"))
                return sems[k]
            return take

        m = dict(
            xs=sb("xs", [P, T, D]), h=sb("h", [P, T, H1]), tmp=sb("tmp", [P, T, D]), stat=sb("stat", [P, 3, T]),
            sums=sb("sums", [P, T, F2]), z=sb("z", [P, T]), deg=sb("deg", [P, T]), coef=sb("coef", [P, T]),
            h3=sb("h3", [P, T, H3], BF16),
            ident=sb("ident", [P, P]), W=sb("W_sb", [P, D]), bias=sb("bias", [P, D]), eps=sb("eps", [P, 1]),
            spread=sb("spread", [WK, WV * (P + 1)], FP16), spread3=sb("spread3", [3, P], FP16),
            bases=sb("bases", [1, SN + 2], I32), basef=sb("basef", [1, SN]),
            src8=sb("src8", [P, SN, SK], I32), dst8=sb("dst8", [P, SN, SK], I32),
            starts=sb("starts", [1, WNP], I32),
            irregular=sb("irregular", [1, 1], I32))
        for name, shape, dt in (
                ("h_dram", [NP, H1], F32), ("acc1_dram", [NP, H1], F32), ("z_dram", [NP, 1], F32), ("acc2_dram", [NP, F2], F32),
                ("rows_dram", [4, E + WE], FP16),
                ("spread_dram", [WK, WV * (P + 1)], FP16), ("h3_dram", [NP, H3], BF16), ("start_dram", [WNP], F32)):
            m[name] = nc.dram_tensor(name, shape, dt).ap()
        prepare(nc, sem, m, x, W, b, src, dst)
        irregular = nc.values_load(m["irregular"][0:1, 0:1], min_val=0, max_val=8 * P)
        sems = []
        with nc.If(irregular > 0):
            general_sums(nc, shared(sems), m, src, dst, edge, 1)
        with nc.Else():
            window_sums(nc, shared(sems), m, src, dst)
        m["acc"] = sb("acc", [P, 2, NP])
        update_nodes(nc, sem, m)
        sems = []
        with nc.If(irregular > 0):
            take = shared(sems)
            general_sums(nc, take, m, src, dst, edge, 2)
            write_result(nc, take, m, out)
        with nc.Else():
            block_sums(nc, shared(sems), m, edge, out)


def prepare(nc, sem, m, x, W, b, src, dst):
    ctx = ExitStack()
    with ctx:
        def sb(name, shape, dt=F32):
            return ctx.enter_context(nc.sbuf_tensor(name, shape, dt))

        srca, dsta = sb("srca", [AR, AC], I32), sb("dsta", [AR, AC], I32)
        hi8, wid, low, part = (sb(k, [AR, AC], I32) for k in ("hi8", "wid", "low", "part"))
        rows = sb("rows", [AR, 4, AC], FP16)
        pad = sb("pad", [4, WE], FP16)
        m_i = sb("m_i", [1, 3, P], I32)
        table = sb("table", [1, WK, WV * (P + 1)], FP16)
        last8 = sb("last8", [1, SN], I32)
        span = sb("span", [1, SN + 1])
        follow = sb("follow", [AR, 1], I32)
        diff = sb("diff", [AR, AC], BF16)
        bad = sb("bad", [P, 6])
        groups = sb("groups", [1, 2, GT * WT])
        extent = sb("extent", [1, 2])
        badsum = sb("badsum", [P, 1])
        ones = sb("ones_col", [P, 1])
        lastrow = sb("lastrow", [AR, AC // LR])
        w8 = sb("w8", [P, 7])
        w8i = sb("w8i", [P, 7], I32)
        junk = sb("junk", [P, 7, LN], BF16)
        row = sb("row", [P, 7])
        rowi = sb("rowi", [P, 7], I32)
        halves = m["sums"][:].rearrange("p t f -> p (t f)")[:, 0:14 * LR].rearrange("p (a c l) -> p a c l", a=2, l=LR)
        looked, lookedf = halves[:, 0].bitcast(I32), halves[:, 1]
        within = sb("within", [P, 7])
        start = sb("start", [P, 7])
        srow = sb("srow", [1, WNP])
        sdiff = sb("sdiff", [1, WN + 1])
        far, near = sb("far", [1, WN]), sb("near", [1, 1])
        ps_last = ctx.enter_context(nc.psum_tensor("ps_last", [P, 8, P], F32))
        ps_bad = ctx.enter_context(nc.psum_tensor("ps_bad", [1, 1], F32))
        dst_in, src_in, x_in, w_in, follow_in, bases_in, row_in, start_out, start_in, table_out, rows_out = (
            sem("a_" + k) for k in ("dst_in", "src_in", "x_in", "w_in", "follow_in", "bases_in", "row_in", "start_out", "start_in", "table_out", "rows_out"))
        blocks_in, group_steps = sem("a_blocks_in"), sem("a_group_steps")
        tail_zero, follow_set, eps_set, ones_set, id_zero, id_done, bad_zero, pad_set, bases_zero, table_zero, iotas = (
            sem("a_" + k) for k in ("tail_zero", "follow_set", "eps_set", "ones_set", "id_zero", "id_done", "bad_zero", "pad_set", "bases_zero", "table_zero", "iotas"))
        x_summed, centered, squared, ssq, root, root_inv, h_done, h_part, h_rest = (
            sem("a_" + k) for k in ("x_summed", "centered", "squared", "ssq", "root", "root_inv", "h_done", "h_part", "h_rest"))
        (last_made, last_spread, row_steps, row_made, key_steps, key_made, low_made, starts_steps, start_made,
         rows_made, table_made, square_steps, squares_made, check_steps, checks_made, bad_added, bad_total) = (
            sem("a_" + k) for k in ("last_made", "last_spread", "row_steps", "row_made", "key_steps", "key_made", "low_made", "starts_steps", "start_made",
                                    "rows_made", "table_made", "square_steps", "squares_made", "check_steps", "checks_made", "bad_added", "bad_total"))
        RC = AC // LR
        total, total_sq, rstd = (m["stat"][:, i, :] for i in range(3))
        hc = m["h"][:, :, 0:D]

        def load_blocks(eng, edges8, v):
            eng.dma_start(edges8[:, 0:SN - 1, :], v[0:(SN - 1) * SE].rearrange("(s p j) -> p s j", p=P, j=SK)).then_inc(blocks_in, 16)
            eng.dma_start(edges8[:, SN - 1, :], v[E - SE:E].rearrange("(p j) -> p j", j=SK)).then_inc(blocks_in, 16)

        with nc.Block() as block:
            @block.sync
            def _(sp):
                sp.dma_start(dsta[:], dst.rearrange("(p c) -> p c", c=AC)).then_inc(dst_in, 16)
                sp.dma_start(m["xs"][:, 0:T - 1, :], x[0:(T - 1) * P, :].rearrange("(t p) f -> p t f", p=P)).then_inc(x_in, 16)
                sp.wait_ge(tail_zero, 1)
                sp.dma_start(m["xs"][0:TAIL, T - 1, :], x[(T - 1) * P:N, :]).then_inc(x_in, 16)
                sp.dma_start(srca[:], src.rearrange("(p c) -> p c", c=AC)).then_inc(src_in, 16)
                sp.wait_ge(follow_set, 1)
                sp.dma_start(follow[0:AR - 1, :], dst.rearrange("(p c) -> p c", c=AC)[1:AR, 0:1], allow_slow_non_contiguous=True).then_inc(follow_in, 16)
                sp.dma_start(m["W"][0:D, :], W[D:F2, :]).then_inc(w_in, 16)
                sp.dma_start(m["W"][D:F2, :], W[0:D, :]).then_inc(w_in, 16)
                sp.dma_start(m["bias"][:], b.rearrange("(o f) -> o f", o=1).to_broadcast([P, D])).then_inc(w_in, 16)
                first = dst[0:(SN - 1) * SE].rearrange("(o s k) -> o s k", o=1, k=SE)
                sp.dma_start(m["bases"][:, 2:SN + 1], first[:, :, 0], allow_slow_non_contiguous=True).then_inc(bases_in, 16)
                sp.dma_start(m["bases"][:, SN + 1:SN + 2], dst[E - SE:E - SE + 1].rearrange("(o s) -> o s", o=1)).then_inc(bases_in, 16)
                sp.dma_start(last8[:, 0:SN - 1], first[:, :, SE - 1], allow_slow_non_contiguous=True).then_inc(bases_in, 16)
                sp.dma_start(last8[:, SN - 1:SN], dst[E - 1:E].rearrange("(o s) -> o s", o=1)).then_inc(bases_in, 16)
                sp.wait_ge(pad_set, 1)
                sp.dma_start(m["rows_dram"][:, E:E + WE], pad[:]).then_inc(rows_out, 16)
                sp.wait_ge(rows_made, 2)
                for k in (0, 3):
                    sp.dma_start(m["rows_dram"][k, 0:E].rearrange("(p c) -> p c", c=AC), rows[:, k, :]).then_inc(rows_out, 16)
                sp.wait_ge(start_made, 1)
                sp.dma_start(m["start_dram"].rearrange("(c p) -> p c", p=P), start[:], allow_slow_non_contiguous=True).then_inc(start_out, 16)
                sp.wait_ge(start_out, 16)
                sp.dma_start(srow[:], m["start_dram"].rearrange("(o c) -> o c", o=1)).then_inc(start_in, 16)
                sp.wait_ge(start_in, 16)
                load_blocks(sp, m["src8"], src)
                sp.wait_ge(table_made, 5 + 3 * WV)
                sp.dma_start(m["spread_dram"].rearrange("(o k) c -> o k c", o=1), table[:]).then_inc(table_out, 16)
                sp.wait_ge(table_out, 16)
                sp.dma_start(m["spread"][:], m["spread_dram"]).then_inc(rows_out, 16)
                sp.dma_start(m["spread3"][:], m["spread_dram"][0:3, 0:P]).then_inc(rows_out, 16)
                sp.wait_ge(rows_made, 4)
                for k in (1, 2):
                    sp.dma_start(m["rows_dram"][k, 0:E].rearrange("(p c) -> p c", c=AC), rows[:, k, :]).then_inc(rows_out, 16)
                sp.wait_ge(rows_out, 112)
                sp.wait_ge(blocks_in, 64)
                sp.wait_ge(w_in, 48)

            @block.gpsimd
            def _(pool):
                nc.gpsimd.memset(m["xs"][:, T - 1, :], 0.0).then_inc(tail_zero, 1)
                nc.gpsimd.memset(follow[:], 1 << 20).then_inc(follow_set, 1)
                nc.gpsimd.iota(w8i[:], [[P * WD, 7]], base=0, channel_multiplier=WD).then_inc(iotas, 1)
                nc.gpsimd.memset(m["ident"][:], 0.0).then_inc(id_zero, 1)
                pool.wait_ge(id_zero, 1)
                nc.gpsimd.affine_select(out=m["ident"][:], in_=m["ident"][:], compare_op=ALU.not_equal, fill=1.0,
                                        base=0, pattern=[[-1, P]], channel_multiplier=1).then_inc(id_done, 1)
                nc.gpsimd.memset(m["eps"][:], EPS).then_inc(eps_set, 1)
                nc.gpsimd.memset(m["h"][:, :, D:H1], 1.0).then_inc(ones_set, 1)
                nc.gpsimd.memset(m["h3"][:, :, H1 + D:2 * H1], 0.0).then_inc(ones_set, 1)
                nc.gpsimd.memset(ones[:], 1.0).then_inc(bad_zero, 1)
                nc.gpsimd.memset(bad[:], 0.0).then_inc(bad_zero, 1)
                nc.gpsimd.memset(m["bases"][:, 0:2], 0).then_inc(bases_zero, 1)
                nc.gpsimd.memset(pad[:], -1.0).then_inc(pad_set, 1)
                nc.gpsimd.iota(m_i[:, 0, :], [[1, P]], base=0, channel_multiplier=0).then_inc(iotas, 1)
                pool.wait_ge(row_made, 1)
                for c in range(7):
                    pool.indirect_dma_start(looked[:, c, :], None, dst.rearrange("(r c) -> r c", c=LR), bass.IndirectOffsetOnAxis(rowi[:, c:c + 1].bitcast(U32), 0)).then_inc(row_in, 16)
                nc.gpsimd.memset(table[:], 0.0).then_inc(table_zero, 1)
                pool.wait_ge(h_part, 1)
                nc.gpsimd.tensor_tensor(m["tmp"][:], hc, m["h3"][:, :, 0:D], ALU.subtract).then_inc(h_rest, 1)
                pool.wait_ge(h_part, 2)
                nc.gpsimd.tensor_tensor(m["tmp"][:], m["tmp"][:], m["h3"][:, :, H1:H1 + D], ALU.subtract).then_inc(h_rest, 1)

            @block.vector
            def _(v):
                v.wait_ge(dst_in, 16)
                nc.vector.tensor_copy(lastrow[:], dsta[:].rearrange("p (r c) -> p r c", c=LR)[:, :, LR - 1]).then_inc(last_made, 1)
                v.wait_ge(iotas, 1)
                nc.vector.tensor_copy(w8[:], w8i[:]).then_inc(row_steps, 1)
                v.wait_ge(row_steps, 1)
                v.wait_ge(last_spread, 1)
                for c in range(7):
                    last = nc.vector.tensor_scalar(junk[:, c, 0:RC * AR].rearrange("p (r c) -> p r c", c=AR), ps_last[:, 0:RC, 0:AR], w8[:, c:c + 1], None, ALU.is_lt, ALU.add, accum_out=row[:, c:c + 1])
                last.then_inc(row_steps, 1)
                v.wait_ge(row_steps, 2)
                nc.vector.tensor_scalar(row[:], row[:], float(LN - 1), None, ALU.min).then_inc(row_steps, 1)
                v.wait_ge(row_steps, 3)
                nc.vector.tensor_copy(rowi[:], row[:]).then_inc(row_made, 1)
                v.wait_ge(x_in, 32)
                nc.vector.reduce_sum(total, m["xs"][:], AX.X).then_inc(x_summed, 1)
                v.wait_ge(x_summed, 1)
                nc.vector.scalar_tensor_tensor(out=hc, in0=total.unsqueeze(2).to_broadcast([P, T, D]), scalar=-1.0 / D, in1=m["xs"][:],
                                               op0=ALU.mult, op1=ALU.add).then_inc(centered, 1)
                v.wait_ge(src_in, 16)
                nc.vector.tensor_scalar(low[:], srca[:], P - 1, None, ALU.bitwise_and).then_inc(low_made, 1)
                nc.vector.tensor_scalar(wid[:], dsta[:], (KM - 1) * WD, 6, ALU.bitwise_and, ALU.logical_shift_left).then_inc(key_steps, 1)
                nc.vector.tensor_scalar(hi8[:], srca[:], 7, 3, ALU.logical_shift_right, ALU.logical_shift_left).then_inc(key_steps, 1)
                v.wait_ge(key_steps, 1)
                nc.vector.scalar_tensor_tensor(out=part[:], in0=dsta[:], scalar=WD - 1, in1=wid[:], op0=ALU.bitwise_and, op1=ALU.bitwise_or).then_inc(key_steps, 1)
                v.wait_ge(key_steps, 3)
                nc.vector.tensor_tensor(part[:], part[:], hi8[:], ALU.bitwise_or).then_inc(key_made, 1)
                v.wait_ge(squared, 1)
                nc.vector.reduce_sum(total_sq, m["tmp"][:], AX.X).then_inc(ssq, 1)
                v.wait_ge(row_in, 112)
                nc.vector.tensor_copy(lookedf, looked).then_inc(starts_steps, 1)
                v.wait_ge(starts_steps, 1)
                for c in range(7):
                    last = nc.vector.tensor_scalar(junk[:, c, 0:LR], lookedf[:, c, :], w8[:, c:c + 1], None, ALU.is_lt, ALU.add, accum_out=within[:, c:c + 1])
                last.then_inc(starts_steps, 1)
                v.wait_ge(starts_steps, 2)
                nc.vector.scalar_tensor_tensor(out=start[:], in0=row[:], scalar=float(LR), in1=within[:], op0=ALU.mult, op1=ALU.add).then_inc(start_made, 1)
                v.wait_ge(root, 1)
                nc.vector.reciprocal(rstd, total).then_inc(root_inv, 1)
                v.wait_ge(root_inv, 1)
                nc.vector.scalar_tensor_tensor(out=hc, in0=hc, scalar=0.0, in1=rstd.unsqueeze(2).to_broadcast([P, T, D]),
                                               op0=ALU.max, op1=ALU.mult).then_inc(h_done, 1)
                v.wait_ge(key_made, 1)
                nc.vector.tensor_tensor(wid[:], low[:], low[:], ALU.mult).then_inc(square_steps, 1)
                v.wait_ge(square_steps, 1)
                nc.vector.tensor_scalar(hi8[:], wid[:], 0x3F00, None, ALU.bitwise_and).then_inc(squares_made, 1)
                nc.vector.tensor_scalar(wid[:], wid[:], 0xFF, None, ALU.bitwise_and).then_inc(squares_made, 1)
                v.wait_ge(iotas, 2)
                v.wait_ge(table_zero, 1)
                nc.vector.tensor_tensor(m_i[:, 1, :], m_i[:, 0, :], m_i[:, 0, :], ALU.mult).then_inc(table_made, 1)
                v.wait_ge(table_made, 1)
                nc.vector.tensor_scalar(m_i[:, 2, :], m_i[:, 1, :], 0x3F00, None, ALU.bitwise_and).then_inc(table_made, 1)
                nc.vector.tensor_scalar(m_i[:, 1, :], m_i[:, 1, :], 0xFF, None, ALU.bitwise_and).then_inc(table_made, 1)
                for j in range(WV):
                    nc.vector.tensor_scalar(table[:, 4 * j, j * P:(j + 1) * P], m_i[:, 0, :], 2.0, None, ALU.mult).then_inc(table_made, 1)
                    nc.vector.memset(table[:, 4 * j + 1:4 * j + 3, j * P:(j + 1) * P], -1.0).then_inc(table_made, 1)
                    nc.vector.memset(table[:, 4 * j + 3, WV * P + j:WV * P + j + 1], 1.0).then_inc(table_made, 1)
                v.wait_ge(table_made, 3)
                rest = [a.unsqueeze(1).to_broadcast([1, WV, P]) for a in (m_i[:, 2, :], m_i[:, 1, :])]
                nc.vector.tensor_scalar(table[:, WK - 2, 0:WV * P].rearrange("o (j m) -> o j m", m=P), rest[0], -1.0, None, ALU.mult).then_inc(table_made, 1)
                nc.vector.tensor_scalar(table[:, WK - 1, 0:WV * P].rearrange("o (j m) -> o j m", m=P), rest[1], -1.0, 1.0, ALU.mult, ALU.add).then_inc(table_made, 1)
                v.wait_ge(start_in, 16)
                nc.vector.tensor_copy(m["starts"][:], srow[:]).then_inc(checks_made, 1)
                nc.vector.tensor_tensor(sdiff[:, 0:WN], srow[:, 1:WN + 1], srow[:, 0:WN], ALU.subtract).then_inc(check_steps, 1)
                nc.vector.tensor_scalar(far[:], srow[:, KM:WN + KM], float(E), float(WE), ALU.is_ge, ALU.mult).then_inc(check_steps, 1)
                v.wait_ge(check_steps, 1)
                nc.vector.tensor_reduce(sdiff[:, WN:WN + 1], sdiff[:, 0:WN], AX.X, ALU.max).then_inc(check_steps, 1)
                v.wait_ge(check_steps, 2)
                nc.vector.tensor_tensor(far[:], far[:], srow[:, KM:WN + KM], ALU.add).then_inc(check_steps, 1)
                v.wait_ge(bad_zero, 2)
                v.wait_ge(check_steps, 3)
                nc.vector.tensor_scalar(bad[0:1, 1:2], sdiff[:, WN:WN + 1], float(WE), None, ALU.is_gt).then_inc(checks_made, 1)
                v.wait_ge(check_steps, 4)
                nc.vector.tensor_tensor(far[:], far[:], srow[:, 0:WN], ALU.subtract).then_inc(check_steps, 1)
                v.wait_ge(check_steps, 5)
                nc.vector.tensor_reduce(near[:], far[:], AX.X, ALU.min).then_inc(check_steps, 1)
                v.wait_ge(check_steps, 6)
                nc.vector.tensor_scalar(bad[0:1, 3:4], near[:], float(WE), None, ALU.is_lt).then_inc(checks_made, 1)
                for k, ahead in enumerate((GD // WD, WT)):
                    nc.vector.tensor_tensor(groups[:, k, :], srow[:, ahead:GT * WT + ahead], srow[:, 0:GT * WT], ALU.subtract).then_inc(group_steps, 1)
                v.wait_ge(group_steps, 2)
                nc.vector.tensor_reduce(extent[:, 0:1], groups[:, 0, :], AX.X, ALU.max).then_inc(group_steps, 1)
                nc.vector.tensor_reduce(extent[:, 1:2], groups[:, 1, :], AX.X, ALU.min).then_inc(group_steps, 1)
                v.wait_ge(group_steps, 4)
                nc.vector.tensor_scalar(bad[0:1, 4:5], extent[:, 0:1], float(GE), None, ALU.is_gt).then_inc(checks_made, 1)
                nc.vector.tensor_scalar(bad[0:1, 5:6], extent[:, 1:2], float(GE), None, ALU.is_lt).then_inc(checks_made, 1)
                v.wait_ge(bases_in, 64)
                v.wait_ge(bases_zero, 1)
                nc.vector.tensor_tensor(span[:, 0:SN], last8[:], m["bases"][:, 2:SN + 2], ALU.subtract).then_inc(check_steps, 1)
                v.wait_ge(check_steps, 7)
                nc.vector.tensor_reduce(span[:, SN:SN + 1], span[:, 0:SN], AX.X, ALU.max).then_inc(check_steps, 1)
                nc.vector.tensor_scalar(m["bases"][:], m["bases"][:], NP - SW, None, ALU.min).then_inc(check_steps, 1)
                v.wait_ge(check_steps, 9)
                nc.vector.tensor_scalar(bad[0:1, 2:3], span[:, SN:SN + 1], float(SW - 1), None, ALU.is_gt).then_inc(checks_made, 1)
                nc.vector.tensor_copy(m["basef"][:], m["bases"][:, 2:SN + 2]).then_inc(checks_made, 1)
                nc.vector.tensor_tensor(diff[:, 0:AC - 1], dsta[:, 1:AC], dsta[:, 0:AC - 1], ALU.subtract).then_inc(check_steps, 1)
                v.wait_ge(follow_in, 16)
                nc.vector.tensor_tensor(diff[:, AC - 1:AC], follow[:], dsta[:, AC - 1:AC], ALU.subtract).then_inc(check_steps, 1)
                v.wait_ge(check_steps, 11)
                nc.vector.tensor_reduce(badsum[0:AR, :], diff[:], AX.X, ALU.min).then_inc(check_steps, 1)
                v.wait_ge(check_steps, 12)
                nc.vector.tensor_scalar(bad[0:AR, 0:1], badsum[0:AR, :], 0.0, None, ALU.is_lt).then_inc(checks_made, 1)
                v.wait_ge(checks_made, 8)
                nc.vector.reduce_sum(badsum[:], bad[:], AX.X).then_inc(bad_added, 1)
                v.wait_ge(bad_total, 1)
                nc.vector.tensor_copy(m["irregular"][:], ps_bad[:])

            @block.tensor
            def _(pe):
                pe.wait_ge(last_made, 1)
                pe.wait_ge(id_done, 1)
                for r in range(RC):
                    last = nc.tensor.matmul(ps_last[:, r, 0:AR], lastrow[:, r:r + 1].to_broadcast([AR, P]), m["ident"][0:AR, 0:AR], start=True, stop=True)
                last.then_inc(last_spread, 1)
                pe.wait_ge(bad_added, 1)
                nc.tensor.matmul(ps_bad[:], badsum[:], ones[:], start=True, stop=True).then_inc(bad_total, 1)

            @block.scalar
            def _(act):
                act.wait_ge(centered, 1)
                nc.scalar.activation(m["tmp"][:], hc, ACT.Square).then_inc(squared, 1)
                act.wait_ge(low_made, 1)
                nc.scalar.copy(rows[:, 0, :], low[:]).then_inc(rows_made, 1)
                act.wait_ge(row_in, 112)
                load_blocks(act, m["dst8"], dst)
                act.wait_ge(key_made, 1)
                nc.scalar.copy(rows[:, 3, :], part[:]).then_inc(rows_made, 1)
                act.wait_ge(ssq, 1)
                act.wait_ge(eps_set, 1)
                nc.scalar.activation(total, total_sq, ACT.Sqrt, bias=m["eps"][:], scale=1.0 / D).then_inc(root, 1)
                act.wait_ge(h_done, 1)
                act.wait_ge(ones_set, 2)
                nc.scalar.copy(m["h3"][:, :, 0:H1], m["h"][:]).then_inc(h_part, 1)
                act.wait_ge(squares_made, 2)
                nc.scalar.copy(rows[:, 1, :], hi8[:]).then_inc(rows_made, 1)
                nc.scalar.copy(rows[:, 2, :], wid[:]).then_inc(rows_made, 1)
                act.wait_ge(h_rest, 1)
                nc.scalar.copy(m["h3"][:, :, H1:H1 + D], m["tmp"][:]).then_inc(h_part, 1)


def general_sums(nc, sem, m, src, dst, edge, layer):
    with ExitStack() as ctx:
        _general_sums(nc, ctx, sem, m, src, dst, edge, layer)


def _general_sums(nc, ctx, sem, m, src, dst, edge, layer):
    R = H1 if layer == 1 else F2
    n = f"g{layer}_"

    def sb(name, shape, dt=F32):
        return ctx.enter_context(nc.sbuf_tensor(name, shape, dt))

    acc = m["acc1_dram"] if layer == 1 else m["acc2_dram"]
    idx = sb(n + "idx", [GC, 2], I32)
    dstf = sb(n + "dstf", [GC, 1])
    same = sb(n + "same", [GC, GC])
    vals = sb(n + "vals", [GC, R])
    old = sb(n + "old", [GC, R])
    new = sb(n + "new", [GC, R])
    zero = sb(n + "zero", [P, R])
    zsrc = sb(n + "zsrc", [GC, 1])
    dst_row = ctx.enter_context(nc.psum_tensor(n + "dst_row", [GC, GC], F32))
    total = ctx.enter_context(nc.psum_tensor(n + "total", [GC, R], F32))
    names = ["zeroed", "table_out", "acc_zeroed", "acc_written", "idx_in", "edge_in", "rows_in", "dst_cast", "row_ready",
             "same_ready", "vals_ready", "sum_ready", "new_ready", "sums_in",
             "gather_begun", "scatter_begun"]
    s = {k: sem(n + k) for k in names}
    srcv = src.rearrange("(c o) -> c o", o=1)
    dstv = dst.rearrange("(c o) -> c o", o=1)
    edgev = edge.rearrange("e a f -> e (a f)")
    with nc.Block() as block:
        @block.sync
        def _(sp):
            if layer == 1:
                sp.dma_start(m["h_dram"].rearrange("(t p) f -> p t f", p=P), m["h"][:]).then_inc(s["table_out"], 16)
            else:
                sp.dma_start(m["z_dram"].rearrange("(t p) o -> p t o", p=P), m["z"][:].unsqueeze(2), allow_slow_non_contiguous=True).then_inc(s["table_out"], 16)
            sp.wait_ge(s["zeroed"], 1)
            sp.dma_start(acc.rearrange("(t p) f -> p t f", p=P), zero[:].unsqueeze(1).to_broadcast([P, T, R])).then_inc(s["acc_zeroed"], 16)
            sp.wait_ge(s["acc_zeroed"], 16)
            sp.wait_ge(s["table_out"], 16)

            def load(i):
                sp.dma_start(idx[:, 0:1], srcv[bass.ds(i * GC, GC), :]).then_inc(s["idx_in"], 16)
                sp.dma_start(idx[:, 1:2], dstv[bass.ds(i * GC, GC), :]).then_inc(s["idx_in"], 16)
                if layer == 2:
                    sp.dma_start(vals[:], edgev[bass.ds(i * GC, GC), :]).then_inc(s["edge_in"], 16)

            load(0)
            with sp.Fori(1, GN) as i:
                sp.wait_ge(s["acc_written"], 16 * i)
                load(i)
            sp.wait_ge(s["acc_written"], 16 * GN)
            out = m["sums"][:, :, 0:R]
            sp.dma_start(out, acc.rearrange("(t p) f -> p t f", p=P)).then_inc(s["sums_in"], 16)
            sp.wait_ge(s["sums_in"], 16)

        @block.gpsimd
        def _(pool):
            nc.gpsimd.memset(zero[:], 0.0).then_inc(s["zeroed"], 1)
            with pool.Fori(0, GN) as i:
                pool.wait_ge(s["idx_in"], 32 * i + 32)
                pool.sem_inc(s["gather_begun"], 1)
                if layer == 1:
                    pool.indirect_dma_start(vals[:], None, m["h_dram"], bass.IndirectOffsetOnAxis(idx[:, 0:1].bitcast(U32), 0)).then_inc(s["rows_in"], 16)
                else:
                    pool.indirect_dma_start(zsrc[:], None, m["z_dram"], bass.IndirectOffsetOnAxis(idx[:, 0:1].bitcast(U32), 0)).then_inc(s["rows_in"], 16)
                pool.indirect_dma_start(old[:], None, acc, bass.IndirectOffsetOnAxis(idx[:, 1:2].bitcast(U32), 0)).then_inc(s["rows_in"], 16)
                pool.wait_ge(s["new_ready"], i + 1)
                pool.sem_inc(s["scatter_begun"], 1)
                pool.indirect_dma_start(acc, bass.IndirectOffsetOnAxis(idx[:, 1:2].bitcast(U32), 0), new[:], None).then_inc(s["acc_written"], 16)

        @block.vector
        def _(dve):
            with dve.Fori(0, GN) as i:
                dve.wait_ge(s["idx_in"], 32 * i + 32)
                nc.vector.tensor_copy(dstf[:], idx[:, 1:2]).then_inc(s["dst_cast"], 1)
                dve.wait_ge(s["row_ready"], i + 1)
                nc.vector.tensor_scalar(same[:], dst_row[:], dstf[:], None, ALU.is_equal).then_inc(s["same_ready"], 1)
                dve.wait_ge(s["rows_in"], 32 * i + 32)
                if layer == 2:
                    dve.wait_ge(s["edge_in"], 16 * i + 16)
                    nc.vector.scalar_tensor_tensor(out=vals[:, 0:D], in0=vals[:, D:F2], scalar=zsrc[:], in1=vals[:, 0:D],
                                                   op0=ALU.mult, op1=ALU.add).then_inc(s["vals_ready"], 1)
                dve.wait_ge(s["sum_ready"], i + 1)
                nc.vector.tensor_tensor(new[:], total[:], old[:], ALU.add).then_inc(s["new_ready"], 1)

        @block.tensor
        def _(pe):
            with pe.Fori(0, GN) as i:
                pe.wait_ge(s["dst_cast"], i + 1)
                nc.tensor.matmul(dst_row[:], dstf[:].to_broadcast([GC, GC]), m["ident"][0:GC, 0:GC], start=True, stop=True).then_inc(s["row_ready"], 1)
                pe.wait_ge(s["same_ready"], i + 1)
                if layer == 1:
                    pe.wait_ge(s["rows_in"], 32 * i + 32)
                else:
                    pe.wait_ge(s["vals_ready"], i + 1)
                nc.tensor.matmul(total[:], same[:], vals[:], start=True, stop=True).then_inc(s["sum_ready"], 1)


def window_sums(nc, sem, m, src, dst):
    ctx = ExitStack()
    with ctx:
        def sb(name, shape, dt=F32):
            return ctx.enter_context(nc.sbuf_tensor(name, shape, dt))

        iota_i = sb("iota_i", [P, KW], I32)
        iota = sb("iota", [P, KW], FP16)
        rows = sb("w_rows", [WK, WS, P], FP16)
        hot_src = sb("hot_src", [P, OS, WV, P], BF16)
        hot_key = sb("hot_key", [P, OS, WV, KW], BF16)
        counts = sb("counts", [P, 2, T, P], FP16)
        parts = sb("parts", [P, 2, H3])
        ps_counts = [ctx.enter_context(nc.psum_tensor(f"ps_counts{k}", [P, 512], F32)) for k in range(BS)]
        ps_square = [ctx.enter_context(nc.psum_tensor(f"ps_wsq{k}", [P, 512], F32)) for k in range(2)]
        ps_keys = [ctx.enter_context(nc.psum_tensor(f"ps_keys{k}", [P, 512], F32)) for k in range(2)]
        ps_sums = ctx.enter_context(nc.psum_tensor("ps_sums", [P, 512], F32))
        ps_group = ctx.enter_context(nc.psum_tensor("ps_group", [P, 512], F32))
        g_src, g_dst = (sb(k, [P, 2, GV], I32) for k in ("g_src", "g_dst"))
        g_low_i, g_low = sb("g_low_i", [P, 2, GV], I32), sb("g_low", [P, 2, GV])
        g_rows = sb("g_rows", [P, 2, GV, H3], BF16)
        g_hot = sb("g_hot", [P, 4, P], BF16)
        g_parts = sb("g_parts", [P, H3])
        h3_out, g_begun, g_lowered, g_hots, g_out, g_steps, g_added = (sem("w_" + k) for k in ("h3_out", "g_begun", "g_lowered", "g_hots", "g_out", "g_steps", "g_added"))
        g_idx_in, g_rows_in = ([sem(f"w_{k}{b}") for b in range(2)] for k in ("g_idx_in", "g_rows_in"))
        g_summed = sem("w_g_summed")
        iotas, iota_cast, dve_parts, h3_made = (sem("w_" + k) for k in ("iotas", "iota_cast", "dve_parts", "h3_made"))
        ones_set, rows_begun = sem("w_ones_set"), sem("w_rows_begun")
        rows_in = [sem(f"w_rows_in{k}") for k in range(WS)]
        squared, src_hot, key_hot = sem("w_squared"), sem("w_src_hot"), sem("w_key_hot")
        counted, counts_out, summed, sums_out, parts_used = (sem(k) for k in ("w_counted", "w_counts_out", "w_summed", "w_sums_out", "w_parts_used"))

        def starts_at(eng, g, n, last):
            return nc.values_load_multi_w_load_instructions(
                m["starts"][0:1, bass.ds(g, n)], engines=[eng], min_val=0, max_val=last,
                skip_runtime_bounds_check_because="a start counts edges, of which there are E, and a group's GE fit behind it")[1]

        with nc.Block() as block:
            @block.sync
            def _(sp):
                sp.sem_inc(squared, WS)
                sp.wait_ge(ones_set, 1)
                with sp.Fori(0, NW * WT, WS) as g:
                    starts = starts_at(mybir.EngineType.SP, g + GT * WT, WS, E)
                    for k in range(WS):
                        sp.wait_ge(squared, g + k + 1)
                        sp.sem_inc(rows_begun, 1)
                        sp.dma_start(rows[0:4 * WV, k, :], m["rows_dram"][:, bass.ds(starts[k], WE)].rearrange("r (j p) -> j r p", p=P)).then_inc(rows_in[k], 16)

            @block.gpsimd
            def _(pool):
                nc.gpsimd.memset(rows[:], 1.0).then_inc(ones_set, 1)
                nc.gpsimd.iota(iota_i[:], [[1, KW]], base=0, channel_multiplier=0).then_inc(iotas, 1)
                pool.wait_ge(h3_made, 1)
                for k in range(T // TG):
                    pool.wait_ge(squared, WS + 2 * k + 2)
                    pool.dma_start(m["h3_dram"].rearrange("(t p) f -> p t f", p=P)[:, k * TG:(k + 1) * TG, :], m["h3"][:, k * TG:(k + 1) * TG, :]).then_inc(h3_out, 16)
                pool.wait_ge(h3_out, 16 * (T // TG))

                with pool.Fori(0, NG, 2) as g:
                    starts = starts_at(mybir.EngineType.Pool, g * (GD // WD), 2 * (GD // WD), E - GE)
                    for b in range(2):
                        pool.wait_ge(g_summed, (g + b + 1) * GV)
                        pool.sem_inc(g_begun, 1)
                        for to, v in ((g_src, src), (g_dst, dst)):
                            pool.dma_start(to[:, b, :], v[bass.ds(starts[b * (GD // WD)], GE)].rearrange("(p c) -> p c", c=GV)).then_inc(g_idx_in[b], 16)
                        pool.wait_ge(g_idx_in[b], 16 * g + 32)
                        pool.sem_inc(g_begun, 1)
                        for c in range(GV):
                            pool.indirect_dma_start(g_rows[:, b, c, :], None, m["h3_dram"], bass.IndirectOffsetOnAxis(g_src[:, b, c:c + 1].bitcast(U32), 0)).then_inc(g_rows_in[b], 16)

            @block.vector
            def _(dve):
                dve.sem_inc(counted, OS)
                dve.wait_ge(iotas, 1)
                nc.vector.tensor_copy(iota[:], iota_i[:]).then_inc(iota_cast, 1)
                dve.wait_ge(iota_cast, 1)

                def add_parts(t, half):
                    dve.wait_ge(sums_out, t + 3)
                    p = parts[:, half, :]
                    nc.vector.tensor_tensor(p[:, H1:H1 + D], p[:, H1:H1 + D], p[:, 2 * H1:H3], ALU.add).then_inc(dve_parts, 1)
                    dve.wait_ge(dve_parts, t + 1)
                    nc.vector.tensor_tensor(m["sums"][:, bass.ds(t + GT, 1), 0:H1], parts[:, half:half + 1, 0:H1], parts[:, half:half + 1, H1:2 * H1], ALU.add).then_inc(parts_used, 1)

                def group_dsts(u, q):
                    dve.wait_ge(g_idx_in[q % 2], 32 * (2 * u + q // 2) + 32)
                    nc.vector.tensor_scalar(g_low_i[:, q % 2, :], g_dst[:, q % 2, :], P - 1, None, ALU.bitwise_and).then_inc(g_lowered, 1)
                    dve.wait_ge(g_lowered, (QG * u + q) * 2 + 1)
                    nc.vector.tensor_copy(g_low[:, q % 2, :], g_low_i[:, q % 2, :]).then_inc(g_lowered, 1)
                    dve.wait_ge(g_lowered, (QG * u + q) * 2 + 2)

                def group_hot(u, q, i):
                    dve.wait_ge(g_summed, (QG * u + q) * GV + (i + 1 + 2 * GV - 4))
                    nc.vector.tensor_scalar(g_hot[:, (q * GV + i) % 4, :], iota[:, 0:P], g_low[:, q % 2, i:i + 1], None, ALU.is_equal).then_inc(g_hots, 1)

                def group_add(u, q):
                    rows_q = slice(q * GD, (q + 1) * GD)
                    dve.wait_ge(g_out, (QG * u + q) + 2)
                    p = g_parts[rows_q, :]
                    nc.vector.tensor_tensor(p[:, H1:H1 + D], p[:, H1:H1 + D], p[:, 2 * H1:H3], ALU.add).then_inc(g_steps, 1)
                    dve.wait_ge(g_steps, (QG * u + q) + 1)
                    nc.vector.tensor_tensor(m["sums"][rows_q, bass.ds(u, 1), 0:H1], p[:, 0:H1].unsqueeze(1), p[:, H1:2 * H1].unsqueeze(1), ALU.add).then_inc(g_added, 1)

                def one_hots(t, half, u=None, q=None, first=False):
                    for i in range(WT):
                        dve.wait_ge(squared, t * WT + (i + 1 + WS))
                        dve.wait_ge(counted, t * WT + (i + 1))
                        for j in range(WV):
                            last = nc.vector.tensor_scalar(hot_key[:, i % OS, j, :], iota[:], float(i % KM * KS),
                                                           ps_keys[i % 2][:, j:j + 1], ALU.add, ALU.is_equal)
                        last.then_inc(key_hot, 1)
                        if q is not None:
                            if i == 0:
                                group_dsts(u, q)
                            if i < GV:
                                group_hot(u, q, i)
                            if i == GV + 4:
                                group_add(u, q)
                        if i == GV + 1 and not first:
                            add_parts(t - 2, half)

                one_hots(0, 0, first=True)
                one_hots(1, 1, first=True)
                with dve.Fori(0, GT) as u:
                    for q in range(QG):
                        one_hots(u * QG + (q + 2), q % 2, u, q)
                one_hots(NW - 2, 0)
                one_hots(NW - 1, 1)
                add_parts(NW - 2, 0)
                add_parts(NW - 1, 1)

            @block.tensor
            def _(pe):
                pe.sem_inc(counts_out, BS)
                pe.sem_inc(sums_out, 2)
                pe.sem_inc(g_summed, 2 * GV)
                pe.sem_inc(g_out, 1)
                pe.sem_inc(src_hot, 2)
                pe.sem_inc(key_hot, 2)

                def square(t, i):
                    k = i % WS
                    pe.wait_ge(rows_in[k], t * (WT // WS * 16) + (i // WS + 1) * 16)
                    pe.wait_ge(src_hot, t * WT + (i + 1))
                    pe.wait_ge(key_hot, t * WT + (i + 1))
                    nc.tensor.matmul(ps_square[i % 2][:, 0:WE], rows[:, k, :], m["spread"][:, 0:WE], start=True, stop=True)
                    nc.tensor.matmul(ps_keys[i % 2][:, 0:WV], rows[:, k, :], m["spread"][:, WE:WE + WV], start=True, stop=True).then_inc(squared, 1)

                def product(t, half, i):
                    for c in range((i - 1) * T // (WT - 1), i * T // (WT - 1)):
                        last = nc.tensor.matmul(ps_sums[:, 0:H3], counts[:, half, c, :], m["h3"][:, c, :], start=(c == 0), stop=(c == T - 1))
                    if i == WT - 1:
                        last.then_inc(summed, 1)

                def product_waits(t):
                    pe.wait_ge(counts_out, t * WT + (WT + BS))
                    pe.wait_ge(sums_out, t + 2)

                def group_sum(u, q, i):
                    if i == 0:
                        pe.wait_ge(g_rows_in[q % 2], 16 * GV * (2 * u + q // 2) + 16 * GV)
                        pe.wait_ge(g_out, QG * u + (q + 1))
                    pe.wait_ge(g_hots, (QG * u + q) * GV + (i + 1))
                    nc.tensor.matmul(ps_group[:, 0:H3], g_hot[:, (q * GV + i) % 4, :], g_rows[:, q % 2, i, :], start=(i == 0), stop=(i == GV - 1)).then_inc(g_summed, 1)

                def count(t, half, u=None, q=None, first=False, final=False):
                    for i in range(WT):
                        if not (final and i >= WT - 2):
                            square(t + (i + 2) // WT, (i + 2) % WT)
                        pe.wait_ge(src_hot, t * WT + (i + 1 + 2))
                        pe.wait_ge(key_hot, t * WT + (i + 1 + 2))
                        pe.wait_ge(counts_out, t * WT + (i + 1))
                        for j in range(WV):
                            last = nc.tensor.matmul(ps_counts[i % BS][:, 0:KW], hot_src[:, i % OS, j, :], hot_key[:, i % OS, j, :], start=(j == 0), stop=(j == WV - 1))
                        last.then_inc(counted, 1)
                        if q is not None and 1 <= i <= GV:
                            group_sum(u, q, i - 1)
                        if i >= 1 and not first:
                            if i == 1:
                                product_waits(t - 1)
                            product(t - 1, 1 - half, i)

                square(0, 0)
                square(0, 1)
                count(0, 0, first=True)
                pe.wait_ge(h3_made, 1)
                count(1, 1)
                with pe.Fori(0, GT) as u:
                    for q in range(QG):
                        count(u * QG + (q + 2), q % 2, u, q)
                count(NW - 2, 0)
                count(NW - 1, 1, final=True)
                product_waits(NW - 1)
                for i in range(1, WT):
                    product(NW - 1, 1, i)

            @block.scalar
            def _(act):
                act.sem_inc(summed, 2)
                act.sem_inc(parts_used, 2)
                act.sem_inc(g_added, 1)
                nc.scalar.copy(m["h3"][:, :, 2 * H1:H3], m["tmp"][:]).then_inc(h3_made, 1)

                def sums_to_sbuf(t, half):
                    act.wait_ge(summed, t + 3)
                    act.wait_ge(parts_used, t + 1)
                    nc.scalar.copy(parts[:, half, :], ps_sums[:, 0:H3]).then_inc(sums_out, 1)

                def group_to_sbuf(u, q):
                    rows_q = slice(q * GD, (q + 1) * GD)
                    act.wait_ge(g_summed, (QG * u + q) * GV + 3 * GV)
                    act.wait_ge(g_added, QG * u + (q + 1))
                    nc.scalar.copy(g_parts[rows_q, :], ps_group[rows_q, 0:H3]).then_inc(g_out, 1)

                def src_one_hot(t, i):
                    act.wait_ge(squared, t * WT + (i + 1 + WS))
                    act.wait_ge(counted, t * WT + (i + 1))
                    nc.scalar.activation(hot_src[:, i % OS, :, :], ps_square[i % 2][:, 0:WE].rearrange("p (j c) -> p j c", c=P), ACT.Relu).then_inc(src_hot, 1)

                def counts_to_sbuf(t, half, u=None, q=None, first=False, final=False):
                    act.wait_ge(summed, t + 1)
                    for i in range(WT):
                        if not (final and i >= WT - 2):
                            src_one_hot(t + (i + 2) // WT, (i + 2) % WT)
                        if i == 0 and not first:
                            sums_to_sbuf(t - 2, half)
                        act.wait_ge(counted, t * WT + (i + 1 + OS))
                        nc.scalar.copy(counts[:, half, :, i * WD:(i + 1) * WD], ps_counts[i % BS][:, 0:KW].rearrange("p (c d) -> p c d", d=WD)).then_inc(counts_out, 1)
                        if q is not None and i == GV + 1:
                            group_to_sbuf(u, q)

                src_one_hot(0, 0)
                src_one_hot(0, 1)
                counts_to_sbuf(0, 0, first=True)
                counts_to_sbuf(1, 1, first=True)
                with act.Fori(0, GT) as u:
                    for q in range(QG):
                        counts_to_sbuf(u * QG + (q + 2), q % 2, u, q)
                counts_to_sbuf(NW - 2, 0)
                counts_to_sbuf(NW - 1, 1, final=True)
                sums_to_sbuf(NW - 2, 0)
                sums_to_sbuf(NW - 1, 1)


def block_sums(nc, sem, m, edge, out):
    with ExitStack() as ctx:
        def sb(name, shape, dt=F32):
            return ctx.enter_context(nc.sbuf_tensor(name, shape, dt))

        def ps(name):
            return ctx.enter_context(nc.psum_tensor(name, [P, 512], F32))

        acc = m["acc"]
        et = sb("et", [P, ER, SK, F2])
        square = sb("square", [3, ER, SE], FP16)
        part_i = sb("part_i", [P, 1], I32)
        part_f, bias1 = sb("part_f", [P, 1]), sb("bias1", [P, 1])
        iota_i = sb("iota64_i", [P, SW], I32)
        iota = sb("iota64", [P, SW])
        ones1 = sb("ones1", [1, P])
        rel = m["tmp"][:].rearrange("p t f -> p (t f)")[:, 0:SN * SK].rearrange("p (s j) -> p s j", j=SK)
        tile_of = sb("tile_of", [P, SN, SK], BF16)
        zpart = sb("zpart", [P, 3, T], BF16)
        zrest = sb("zrest", [P, 2, T])
        hot_lo = sb("hot_lo", [P, 2, SE], BF16)
        hot_dst = m["sums"][:].rearrange("p t f -> p (t f)")[:, 0:EH * SK * 2 * SW].rearrange("p (b j f) -> p b j f", j=SK, f=2 * SW)
        pick = m["h3"][:].rearrange("p t f -> p (t f)").bitcast(F32)[:, 0:4 * SK * T].rearrange("p (a b j t) -> p a b j t", a=2, b=2, t=T)
        mask, picked = pick[:, 0], pick[:, 1]
        zsrc = sb("zsrc", [P, 2, SK])
        ps_square = [[ps(f"ps_square{i}{k}") for k in range(2)] for i in range(2)]
        ps_z = [ps(f"ps_z{i}") for i in range(2)]
        ps_acc = [ps(f"ps_acc{i}") for i in range(2)]
        consts, setup, base_spread, rel_made, rel_masked = (sem("b_" + k) for k in ("consts", "setup", "base_spread", "rel_made", "rel_masked"))
        rest, h_scaled = sem("b_rest"), sem("b_h_scaled")
        edges_in = [sem(f"b_edges_in{k}") for k in range(ER)]
        squares_in = [sem(f"b_squares_in{k}") for k in range(ER)]
        squared, mask_made, picked_made, z_ready, hots_made = (sem("b_" + k) for k in ("squared", "mask_made", "picked_made", "z_ready", "hots_made"))
        lo_made, z_spread, q_made, summed, acc_added = (sem("b_" + k) for k in ("lo_made", "z_spread", "q_made", "summed", "acc_added"))
        rows = edge.rearrange("e a f -> e (a f)")

        def first_edge(s):
            return E - SE if isinstance(s, int) and s == SN - 1 else s * SE

        def blocks(eng, step, lag_before, lag_after):
            for s in range(-lag_before, ER):
                step(s, s % ER)
            with eng.Fori(ER, SN - 1 - ER, ER) as s0:
                for r in range(ER):
                    step(s0 + r, r)
            for s in range(SN - 2, SN + lag_after):
                step(s, s % ER)

        def within(s):
            return not isinstance(s, int) or 0 <= s < SN

        with nc.Block() as block:
            @block.sync
            def _(sp):
                sp.sem_inc(summed, ER)

                def load(s, r):
                    sp.wait_ge(summed, s + 1)
                    sp.dma_start(square[:, r, :], m["rows_dram"][0:3, bass.ds(first_edge(s), SE)]).then_inc(squares_in[r], 16)
                    sp.dma_start(et[:, r, :, :].rearrange("p j f -> p (j f)"),
                                 rows[bass.ds(first_edge(s), SE), :].rearrange("(p j) f -> p (j f)", j=SK)).then_inc(edges_in[r], 16)

                blocks(sp, load, 0, 0)

            @block.tensor
            def _(pe):
                pe.sem_inc(lo_made, 2)
                pe.sem_inc(q_made, 2)
                pe.sem_inc(acc_added, 2)
                pe.wait_ge(consts, 3)
                nc.tensor.matmul(ps_acc[0][:, 0:SN], ones1[:], m["basef"][:], start=True, stop=True).then_inc(base_spread, 1)
                pe.wait_ge(setup, 7)
                pe.wait_ge(rel_made, 1)

                def spread_squares(s, r):
                    pe.wait_ge(squares_in[r], (s - r) * (16 // ER) + 16)
                    pe.wait_ge(lo_made, s + 1)
                    for k in range(2):
                        last = nc.tensor.matmul(ps_square[r % 2][k][:], m["spread3"][:], square[:, r, k * 512:(k + 1) * 512], start=True, stop=True)
                    last.then_inc(squared, 1)

                def spread_z(s, r):
                    pe.wait_ge(lo_made, s + 3)
                    pe.wait_ge(picked_made, s + 1)
                    for j in range(SK):
                        for k in range(3):
                            last = nc.tensor.matmul(ps_z[r % 2][:, j * T:(j + 1) * T], hot_lo[:, r % 2, j:SE:SK], zpart[:, k, :], start=(k == 0), stop=(k == 2))
                    last.then_inc(z_spread, 1)

                def sum_block(s, r):
                    pe.wait_ge(q_made, s + 3)
                    pe.wait_ge(edges_in[r], (s - r) * (16 // ER) + 16)
                    pe.wait_ge(acc_added, s + 1)
                    for j in range(SK):
                        last = nc.tensor.matmul(ps_acc[r % 2][:, 0:2 * SW], et[:, r, j, :], hot_dst[:, r % EH, j, :], start=(j == 0), stop=(j == SK - 1))
                    last.then_inc(summed, 1)

                def step(s, r):
                    if within(s + 2 if isinstance(s, int) else s):
                        spread_squares(s + 2, (r + 2) % ER)
                    if within(s + 1 if isinstance(s, int) else s):
                        spread_z(s + 1, (r + 1) % ER)
                    if within(s - 1 if isinstance(s, int) else s):
                        sum_block(s - 1, (r - 1) % ER)

                blocks(pe, step, 2, 1)

            @block.scalar
            def _(act):
                act.sem_inc(z_spread, 2)
                act.wait_ge(setup, 7)

                def one_hot(s, r):
                    act.wait_ge(squared, s + 1)
                    act.wait_ge(z_spread, s + 1)
                    for k in range(2):
                        last = nc.scalar.activation(hot_lo[:, r % 2, k * 512:(k + 1) * 512], ps_square[r % 2][k][:], ACT.Relu, bias=bias1[:])
                    last.then_inc(lo_made, 1)

                blocks(act, one_hot, 0, 0)

            @block.vector
            def _(dve):
                dve.sem_inc(picked_made, 2)
                dve.wait_ge(consts, 3)
                nc.vector.tensor_copy(part_f[:], part_i[:]).then_inc(setup, 1)
                nc.vector.tensor_copy(iota[:], iota_i[:]).then_inc(setup, 1)
                nc.vector.tensor_copy(zpart[:, 0, :], m["z"][:]).then_inc(setup, 1)
                dve.wait_ge(setup, 3)
                nc.vector.tensor_tensor(zrest[:, 0, :], m["z"][:], zpart[:, 0, :], ALU.subtract).then_inc(setup, 1)
                nc.vector.tensor_tensor(bias1[:], part_f[:], part_f[:], ALU.mult).then_inc(setup, 1)
                dve.wait_ge(setup, 5)
                nc.vector.tensor_scalar(bias1[:], bias1[:], -1.0, 1.0, ALU.mult, ALU.add).then_inc(setup, 1)
                nc.vector.tensor_copy(zpart[:, 1, :], zrest[:, 0, :]).then_inc(rest, 1)
                dve.wait_ge(rest, 1)
                nc.vector.tensor_tensor(zrest[:, 1, :], zrest[:, 0, :], zpart[:, 1, :], ALU.subtract).then_inc(rest, 1)
                dve.wait_ge(rest, 2)
                nc.vector.tensor_copy(zpart[:, 2, :], zrest[:, 1, :]).then_inc(setup, 1)
                dve.wait_ge(base_spread, 1)
                nc.vector.tensor_tensor(rel, m["dst8"][:], ps_acc[0][:, 0:SN].unsqueeze(2).to_broadcast([P, SN, SK]), ALU.subtract).then_inc(rel_made, 1)
                nc.vector.tensor_scalar(m["src8"][:], m["src8"][:], 7, None, ALU.logical_shift_right).then_inc(rest, 1)
                dve.wait_ge(rest, 3)
                nc.vector.tensor_copy(tile_of[:], m["src8"][:]).then_inc(rest, 1)
                dve.wait_ge(rest, 4)
                dve.wait_ge(rel_masked, 1)

                def pick_z(s, r):
                    h = r % 2
                    nc.vector.tensor_tensor(mask[:, h, :, :], iota[:, 0:T].unsqueeze(1).to_broadcast([P, SK, T]), tile_of[:, bass.ds(s, 1), :].rearrange("p o j -> p (o j)").unsqueeze(2).to_broadcast([P, SK, T]), ALU.is_equal).then_inc(mask_made, 1)
                    dve.wait_ge(mask_made, s + 1)
                    dve.wait_ge(z_spread, s + 3)
                    nc.vector.tensor_tensor(picked[:, h, :, :], mask[:, h, :, :], ps_z[h][:, 0:SK * T].rearrange("p (j t) -> p j t", t=T), ALU.mult).then_inc(picked_made, 1)
                    dve.wait_ge(picked_made, s + 3)
                    dve.wait_ge(q_made, s + 1)
                    nc.vector.reduce_sum(zsrc[:, h, :], picked[:, h, :, :], AX.X).then_inc(z_ready, 1)

                def hot_dsts(s, r):
                    dve.wait_ge(summed, s + 1 + ER - EH)
                    nc.vector.tensor_tensor(hot_dst[:, r % EH, :, 0:SW], iota[:].unsqueeze(1).to_broadcast([P, SK, SW]), rel[:, bass.ds(s, 1), :].rearrange("p o j -> p (o j)").unsqueeze(2).to_broadcast([P, SK, SW]), ALU.is_equal).then_inc(hots_made, 1)

                def add_block(s, r, base):
                    dve.wait_ge(summed, s + 1 + ER)
                    dve.wait_ge(acc_added, s + 2)
                    at = acc[:, :, bass.ds(base, SW)]
                    nc.vector.tensor_tensor(at, at, ps_acc[r % 2][:, 0:2 * SW].rearrange("p (a w) -> p a w", w=SW), ALU.add).then_inc(acc_added, 1)

                def step(s, r, base):
                    if within(s):
                        hot_dsts(s, r)
                        pick_z(s, r)
                    if within(s - 2 if isinstance(s, int) else s):
                        add_block(s - 2, (r - 2) % ER, base)

                def base_of(s, n):
                    return nc.values_load_multi_w_load_instructions(
                        m["bases"][0:1, bass.ds(s, n)], engines=[mybir.EngineType.DVE], min_val=0, max_val=NP - SW,
                        skip_runtime_bounds_check_because="the bases are clamped to this range when they are computed")[1]

                for s in range(ER):
                    step(s, s % ER, base_of(s, 1)[0] if s >= 2 else None)
                with dve.Fori(ER, SN - 1 - ER, ER) as s0:
                    base = base_of(s0, ER)
                    for r in range(ER):
                        step(s0 + r, r, base[r])
                for s in range(SN - 2, SN + 2):
                    step(s, s % ER, base_of(s, 1)[0])

            @block.gpsimd
            def _(pool):
                nc.gpsimd.iota(part_i[:], [[0, 1]], base=0, channel_multiplier=1).then_inc(consts, 1)
                nc.gpsimd.iota(iota_i[:], [[1, SW]], base=0, channel_multiplier=0).then_inc(consts, 1)
                nc.gpsimd.memset(ones1[:], 1.0).then_inc(consts, 1)
                pool.wait_ge(rel_made, 1)
                nc.gpsimd.affine_select(out=rel[:, SN - 1, :], in_=rel[:, SN - 1, :], compare_op=ALU.is_ge, fill=-1.0,
                                        base=-SO, pattern=[[1, SK]], channel_multiplier=SK).then_inc(rel_masked, 1)

                def scale(s, r):
                    if isinstance(s, int) and s < T // TG:
                        tiles = slice(s * TG, (s + 1) * TG)
                        h = m["h"][:, tiles, 0:D]
                        nc.gpsimd.tensor_tensor(h, h, m["coef"][:, tiles].unsqueeze(2).to_broadcast([P, TG, D]), ALU.mult).then_inc(h_scaled, 1)
                        pool.wait_ge(h_scaled, s + 1)
                        nc.gpsimd.tensor_tensor(m["xs"][:, tiles, :], m["xs"][:, tiles, :], h, ALU.add)
                    pool.wait_ge(z_ready, s + 1)
                    pool.wait_ge(hots_made, s + 1)
                    nc.gpsimd.tensor_tensor(hot_dst[:, r % EH, :, SW:2 * SW], hot_dst[:, r % EH, :, 0:SW],
                                            zsrc[:, r % 2, :].unsqueeze(2).to_broadcast([P, SK, SW]), ALU.mult).then_inc(q_made, 1)

                blocks(pool, scale, 0, 0)

        small = sb("small", [P, 1])
        small_set, turned, q_out, den_out, inverted, divided, made, stored = (
            sem("b_" + k) for k in ("small_set", "turned", "q_out", "den_out", "inverted", "divided", "made", "stored"))
        banks = [b for pair in ps_square for b in pair] + ps_z + ps_acc
        groups = [slice(t, min(t + 2, T)) for t in range(0, T, 2)]
        stores = [(first, min(first + 16, T - 1)) for first in range(0, T - 1, 16)]
        with nc.Block() as block:
            @block.tensor
            def _(pe):
                for g, tiles in enumerate(groups):
                    if g >= 8:
                        pe.wait_ge(den_out, g - 7)
                    for t in range(tiles.start, tiles.stop):
                        at = banks[g % 8][:, t % 2 * P:(t % 2 + 1) * P]
                        nc.tensor.matmul(at, acc[:, 0, t * P:(t + 1) * P], m["ident"][:], start=True, stop=False)
                        last = nc.tensor.matmul(at[:, 0:D], acc[:, 1, t * P:(t + 1) * P], m["ident"][:, D:F2], start=False, stop=True)
                    last.then_inc(turned, 1)

            @block.scalar
            def _(act):
                act.wait_ge(small_set, 1)
                for g, tiles in enumerate(groups):
                    n = tiles.stop - tiles.start
                    both = banks[g % 8][:, 0:n * P].rearrange("p (t f) -> p t f", f=P)
                    act.wait_ge(turned, g + 1)
                    nc.scalar.activation(m["sums"][:, tiles, 0:D], both[:, :, 0:D], ACT.Copy, scale=1.0 - BETA).then_inc(q_out, 1)
                    nc.scalar.activation(m["sums"][:, tiles, D:F2], both[:, :, D:F2], ACT.Identity, bias=small[:]).then_inc(den_out, 1)

            @block.vector
            def _(dve):
                for g, tiles in enumerate(groups):
                    q, den = m["sums"][:, tiles, 0:D], m["sums"][:, tiles, D:F2]
                    dve.wait_ge(den_out, g + 1)
                    nc.vector.reciprocal(den, den).then_inc(inverted, 1)
                    dve.wait_ge(q_out, g + 1)
                    dve.wait_ge(inverted, g + 1)
                    nc.vector.tensor_tensor(q, q, den, ALU.mult).then_inc(divided, 1)

            @block.gpsimd
            def _(pool):
                nc.gpsimd.memset(small[:], 1e-6).then_inc(small_set, 1)
                for g, tiles in enumerate(groups):
                    pool.wait_ge(divided, g + 1)
                    nc.gpsimd.tensor_tensor(m["tmp"][:, tiles, :], m["xs"][:, tiles, :], m["sums"][:, tiles, 0:D], ALU.add).then_inc(made, 1)

            @block.sync
            def _(sp):
                for first, end in stores:
                    sp.wait_ge(made, end // 2)
                    sp.dma_start(out[first * P:end * P, :].rearrange("(t p) f -> p t f", p=P), m["tmp"][:, first:end, :]).then_inc(stored, 16)
                sp.wait_ge(made, len(groups))
                sp.dma_start(out[(T - 1) * P:N, :], m["tmp"][0:TAIL, T - 1, :]).then_inc(stored, 16)
                sp.wait_ge(stored, 16 * (len(stores) + 1))


def update_nodes(nc, sem, m):
    with ExitStack() as ctx:
        _update_nodes(nc, ctx, sem, m)


def _update_nodes(nc, ctx, sem, m):
    def sb(name, shape, dt=F32):
        return ctx.enter_context(nc.sbuf_tensor(name, shape, dt))

    G = T // TG
    catT = sb("catT", [P, 2, TG, P])
    rdeg = sb("rdeg", [P, T])
    psT = [ctx.enter_context(nc.psum_tensor(f"psT{k}", [P, 8, P], F32)) for k in range(2)]
    psY = [ctx.enter_context(nc.psum_tensor(f"psY{k}", [P, 8, D], F32)) for k in range(2)]
    deg_done, rdeg_done, n_scaled, h_copied, turned, turned_out, projected, x_updated = (
        sem("u_" + k) for k in ("deg_done", "rdeg_done", "n_scaled", "h_copied", "turned", "turned_out", "projected", "x_updated"))
    x_summed, centered, squared, relued, ssq, root, root_inv, hmax = (
        sem("u_" + k) for k in ("x_summed", "centered", "squared", "relued", "ssq", "root", "root_inv", "hmax"))
    with_bias = sem("u_with_bias")
    total, total_sq, rstd = (m["stat"][:, i, :] for i in range(3))
    cat = m["sums"]
    with nc.Block() as block:
        @block.vector
        def _(dve):
            nc.vector.tensor_copy(m["deg"][:].unsqueeze(2), m["sums"][:, :, D:H1]).then_inc(deg_done, 1)
            dve.wait_ge(deg_done, 1)
            nc.vector.tensor_scalar(rdeg[:], m["deg"][:], 1.0, None, ALU.max).then_inc(rdeg_done, 1)
            dve.wait_ge(rdeg_done, 1)
            nc.vector.reciprocal(rdeg[:], rdeg[:]).then_inc(rdeg_done, 1)
            nc.vector.tensor_scalar(m["coef"][:], m["deg"][:], 0.0, BETA, ALU.is_equal, ALU.max).then_inc(deg_done, 1)
            dve.wait_ge(rdeg_done, 2)
            for g in range(G):
                tiles = slice(g * TG, (g + 1) * TG)
                nc.vector.tensor_tensor(cat[:, tiles, 0:D], cat[:, tiles, 0:D], rdeg[:, tiles].unsqueeze(2).to_broadcast([P, TG, D]), ALU.mult).then_inc(n_scaled, 1)

            def center(g):
                tiles = slice(g * TG, (g + 1) * TG)
                dve.wait_ge(projected, g + 1)
                dve.wait_ge(with_bias, g + 1)
                nc.vector.tensor_tensor(m["xs"][:, tiles, :], m["xs"][:, tiles, :], psY[g % 2][:, 0:TG, :], ALU.add).then_inc(x_updated, 1)
                dve.wait_ge(x_updated, g + 1)
                nc.vector.reduce_sum(total[:, tiles], m["xs"][:, tiles, :], AX.X).then_inc(x_summed, 1)
                dve.wait_ge(x_summed, g + 1)
                nc.vector.scalar_tensor_tensor(out=m["h"][:, tiles, 0:D], in0=total[:, tiles].unsqueeze(2).to_broadcast([P, TG, D]), scalar=-1.0 / D,
                                               in1=m["xs"][:, tiles, :], op0=ALU.mult, op1=ALU.add).then_inc(centered, 1)

            def reduce(g):
                tiles = slice(g * TG, (g + 1) * TG)
                dve.wait_ge(squared, g + 1)
                nc.vector.reduce_sum(total_sq[:, tiles], m["tmp"][:, tiles, :], AX.X).then_inc(ssq, 1)
                dve.wait_ge(relued, g + 1)
                nc.vector.tensor_reduce(m["z"][:, tiles], m["h"][:, tiles, 0:D], AX.X, ALU.max).then_inc(hmax, 1)

            for g in range(G):
                center(g)
                if g >= 1:
                    reduce(g - 1)
            reduce(G - 1)
            dve.wait_ge(root, 1)
            nc.vector.reciprocal(rstd, total).then_inc(root_inv, 1)
            dve.wait_ge(root_inv, 1)
            dve.wait_ge(hmax, G)
            nc.vector.tensor_tensor(m["z"][:], m["z"][:], rstd, ALU.mult).then_inc(hmax, 1)
            nc.vector.tensor_tensor(m["coef"][:], m["coef"][:], rstd, ALU.mult)
            dve.wait_ge(hmax, G + 1)
            nc.vector.tensor_scalar(m["z"][:], m["z"][:], GAMMA, None, ALU.mult)

        @block.tensor
        def _(pe):
            def project(g):
                pe.wait_ge(turned_out, g + 1)
                if g >= 2:
                    pe.wait_ge(x_updated, g - 1)
                for k in range(TG):
                    last = nc.tensor.matmul(psY[g % 2][:, k, :], catT[:, g % 2, k, :], m["W"][:], start=True, stop=True)
                last.then_inc(projected, 1)

            for g in range(G):
                pe.wait_ge(n_scaled, g + 1)
                pe.wait_ge(h_copied, g + 1)
                if g >= 2:
                    pe.wait_ge(turned_out, g - 1)
                for k in range(TG):
                    last = nc.tensor.transpose(psT[g % 2][:, k, :], cat[:, g * TG + k, :], m["ident"][:])
                last.then_inc(turned, 1)
                if g >= 1:
                    project(g - 1)
            project(G - 1)

        @block.scalar
        def _(act):
            act.wait_ge(deg_done, 1)
            for g in range(G):
                tiles = slice(g * TG, (g + 1) * TG)
                nc.scalar.copy(cat[:, tiles, D:F2], m["h"][:, tiles, 0:D]).then_inc(h_copied, 1)

            def square(g):
                tiles = slice(g * TG, (g + 1) * TG)
                act.wait_ge(centered, g + 1)
                nc.scalar.activation(m["tmp"][:, tiles, :], m["h"][:, tiles, 0:D], ACT.Square).then_inc(squared, 1)
                act.wait_ge(squared, g + 1)
                nc.scalar.activation(m["h"][:, tiles, 0:D], m["h"][:, tiles, 0:D], ACT.Relu).then_inc(relued, 1)

            for g in range(G):
                act.wait_ge(turned, g + 1)
                if g >= 2:
                    act.wait_ge(projected, g - 1)
                nc.scalar.copy(catT[:, g % 2], psT[g % 2][:, 0:TG, :]).then_inc(turned_out, 1)
                if g >= 2:
                    square(g - 2)
            square(G - 2)
            square(G - 1)
            act.wait_ge(ssq, G)
            nc.scalar.activation(total, total_sq, ACT.Sqrt, bias=m["eps"][:], scale=1.0 / D).then_inc(root, 1)

        @block.gpsimd
        def _(pool):
            for g in range(G):
                x = m["xs"][:, g * TG:(g + 1) * TG, :]
                nc.gpsimd.tensor_tensor(x, x, m["bias"][:].unsqueeze(1).to_broadcast([P, TG, D]), ALU.add).then_inc(with_bias, 1)
            nc.gpsimd.memset(m["acc"][:], 0.0)


def write_result(nc, sem, m, out):
    den, scaled, with_x, ratio, summed, stored = (sem("r_" + k) for k in ("den", "scaled", "with_x", "ratio", "summed", "stored"))
    q, ac = m["sums"][:, :, 0:D], m["sums"][:, :, D:F2]
    h = m["h"][:, :, 0:D]
    with nc.Block() as block:
        @block.vector
        def _(dve):
            nc.vector.tensor_scalar(ac, ac, 1e-6, None, ALU.add).then_inc(den, 1)
            nc.vector.tensor_tensor(h, h, m["coef"][:].unsqueeze(2).to_broadcast([P, T, D]), ALU.mult).then_inc(scaled, 1)
            dve.wait_ge(den, 1)
            nc.vector.reciprocal(ac, ac).then_inc(den, 1)
            dve.wait_ge(den, 2)
            nc.vector.scalar_tensor_tensor(out=q, in0=q, scalar=1.0 - BETA, in1=ac, op0=ALU.mult, op1=ALU.mult).then_inc(ratio, 1)
            dve.wait_ge(scaled, 1)
            nc.vector.tensor_tensor(h, h, m["xs"][:], ALU.add).then_inc(with_x, 1)
            dve.wait_ge(ratio, 1)
            dve.wait_ge(with_x, 1)
            nc.vector.tensor_tensor(m["tmp"][:], h, q, ALU.add).then_inc(summed, 1)

        @block.sync
        def _(sp):
            sp.wait_ge(summed, 1)
            sp.dma_start(out[0:(T - 1) * P, :].rearrange("(t p) f -> p t f", p=P), m["tmp"][:, 0:T - 1, :]).then_inc(stored, 16)
            sp.dma_start(out[(T - 1) * P:N, :], m["tmp"][0:TAIL, T - 1, :]).then_inc(stored, 16)
            sp.wait_ge(stored, 32)


_INS = ['x', 'src', 'dst', 'edge_attr3_2x64', 'L0_gnn_W', 'L0_gnn_b']


def kernel(**inputs):
    import numpy as _np
    import concourse.bacc as _bacc
    from concourse import mybir as _mybir
    from concourse.bass_utils import run_bass_kernel_spmd as _run

    nc = _bacc.Bacc("TRN2", target_bir_lowering=False, num_devices=1)
    arrays, args = {}, []
    for name in _INS:
        a = _np.ascontiguousarray(inputs[name])
        arrays[f"in_{name}_dram"] = a
        args.append(nc.dram_tensor(f"in_{name}_dram", a.shape, _mybir.dt.from_np(a.dtype), kind="ExternalInput").ap())
    out = nc.dram_tensor("out_0_dram", (N, D), F32, kind="ExternalOutput").ap()
    build(nc, *args, out)
    r = _run(nc, [arrays], core_ids=[0])
    return r.results[0]["out_0_dram"]
```
